# Optimizing a Trainium2 kernel written in Bass

```python
import numpy as np
import jax
import jax.numpy as jnp

def _softmax(x, axis=-1):
    return jax.nn.softmax(x, axis=axis)
def _gelu(x):
    return jax.nn.gelu(x, approximate=True)
def _silu(x):
    return jax.nn.silu(x)
def _sigmoid(x):
    return jax.nn.sigmoid(x)
def _layernorm(x, axis=-1, eps=1e-5):
    m = jnp.mean(x, axis=axis, keepdims=True)
    v = jnp.var(x, axis=axis, keepdims=True)
    return (x - m) / jnp.sqrt(v + eps)
def _scatter_add(tgt, idx, src, axis=0):
    return tgt.at[idx].add(src)
def _segment_sum(src, seg, n):
    return jax.ops.segment_sum(src, seg, n)

kernel_name = 'mk_conv_seq_d1_conv_nchw256_8cfa4f'

def setup_inputs(seed: int = 0):
    np.random.seed(seed)
    _w = jnp.asarray
    def _rec_inputs():
        import jax
        import jax.numpy as jnp
        _gk = jax.random.key(seed)
        x = 7.22e-05 + 1 * jax.random.normal(jax.random.fold_in(_gk, 1), (8, 256, 64, 64), jnp.float32)
        return x
    x = _rec_inputs()
    def _L0_conv_setup():
        import jax, jax.numpy as jnp
        import numpy as np
        DIM = 256
        DSTATE = 64
        DCONV = 3
        HEADDIM = 64
        CHUNK = 256
        NGROUPS = 1
        DINNER = int(2.0 * DIM)
        NHEADS = DINNER // HEADDIM
        CONVDIM = DINNER + 2 * NGROUPS * DSTATE
        DPROJ = 2 * DINNER + 2 * NGROUPS * DSTATE + NHEADS

        def _ssd(X, dA, Bm, Cm, chunk):
            b, l, h, p = X.shape
            n = Bm.shape[-1]
            c = l // chunk
            q = chunk
            Xc = X.reshape(b, c, q, h, p)
            Bc = Bm.reshape(b, c, q, h, n)
            Cc = Cm.reshape(b, c, q, h, n)
            Ac = dA.reshape(b, c, q, h).transpose(0, 3, 1, 2)
            Acs = jnp.cumsum(Ac, axis=-1)
            tri = jnp.tril(jnp.ones((q, q), bool))
            Ldec = jnp.where(tri, jnp.exp(Acs[..., :, None] - Acs[..., None, :]), 0.0)
            Y_diag = jnp.einsum('bcqhn,bcshn,bhcqs,bcshp->bcqhp', Cc, Bc, Ldec, Xc)
            decay_states = jnp.exp(Acs[..., -1:] - Acs)
            states = jnp.einsum('bcqhn,bhcq,bcqhp->bchpn', Bc, decay_states, Xc)
            A_last = jnp.pad(Acs[..., -1], ((0, 0), (0, 0), (1, 0)))
            ccs = jnp.cumsum(A_last, axis=-1)
            tric = jnp.tril(jnp.ones((c + 1, c + 1), bool))
            decay_chunk = jnp.where(tric, jnp.exp(ccs[..., :, None] - ccs[..., None, :]), 0.0)
            states0 = jnp.concatenate([jnp.zeros_like(states[:, :1]), states], axis=1)
            prev = jnp.einsum('bhzc,bchpn->bzhpn', decay_chunk, states0)[:, :-1]
            Y_off = jnp.einsum('bcqhn,bchpn,bhcq->bcqhp', Cc, prev, jnp.exp(Acs))
            return (Y_diag + Y_off).reshape(b, l, h, p)

        def _forward(x, ln_w, ln_b, in_proj_w, conv_w, conv_b, A_log, D, dt_bias, rms_w, out_proj_w):
            Bn, Cd, Hh, Ww = x.shape
            L = Hh * Ww
            mu = jnp.mean(x, axis=1, keepdims=True)
            var = jnp.mean((x - mu) ** 2, axis=1, keepdims=True)
            xn = (x - mu) * jax.lax.rsqrt(var + 1e-05)
            xn = xn * ln_w[None, :, None, None] + ln_b[None, :, None, None]
            zxbcdt = jnp.einsum('bchw,dc->bdhw', xn, in_proj_w)
            z = zxbcdt[:, :DINNER]
            xBC = zxbcdt[:, DINNER:DINNER + CONVDIM]
            dt = zxbcdt[:, DINNER + CONVDIM:]
            xBC = jax.lax.conv_general_dilated(xBC, conv_w, (1, 1), 'SAME', dimension_numbers=('NCHW', 'OIHW', 'NCHW'), feature_group_count=CONVDIM)
            xBC = jax.nn.silu(xBC + conv_b[None, :, None, None])

            def to_seq(t):
                return t.reshape(Bn, t.shape[1], L).transpose(0, 2, 1)
            xBC, dt, z = (to_seq(xBC), to_seq(dt), to_seq(z))
            xs = xBC[..., :DINNER].reshape(Bn, L, NHEADS, HEADDIM)
            Bg = xBC[..., DINNER:DINNER + NGROUPS * DSTATE].reshape(Bn, L, NGROUPS, DSTATE)
            Cg = xBC[..., DINNER + NGROUPS * DSTATE:].reshape(Bn, L, NGROUPS, DSTATE)
            hpg = NHEADS // NGROUPS
            Bm = jnp.repeat(Bg, hpg, axis=2)
            Cm = jnp.repeat(Cg, hpg, axis=2)
            dt = jax.nn.softplus(dt + dt_bias[None, None, :])
            A = -jnp.exp(A_log)
            y = _ssd(xs * dt[..., None], dt * A[None, None, :], Bm, Cm, CHUNK)
            y = y + D[None, None, :, None] * xs
            y = y.reshape(Bn, L, DINNER)
            y = y * jax.nn.silu(z)
            y = y * jax.lax.rsqrt(jnp.mean(y * y, axis=-1, keepdims=True) + 1e-05) * rms_w
            out = jnp.einsum('bld,cd->blc', y, out_proj_w)
            out = out.transpose(0, 2, 1).reshape(Bn, Cd, Hh, Ww)
            return x + out
        key = jax.random.key(seed)
        ks = jax.random.split(key, 8)
        B, H, W = (8, 64, 64)
        return dict(x=jax.random.normal(ks[0], (B, DIM, H, W), jnp.float32), ln_w=jnp.ones((DIM,), jnp.float32), ln_b=jnp.zeros((DIM,), jnp.float32), in_proj_w=jax.random.normal(ks[1], (DPROJ, DIM), jnp.float32) * 0.02, conv_w=jax.random.normal(ks[2], (CONVDIM, 1, DCONV, DCONV), jnp.float32) * 0.1, conv_b=jnp.zeros((CONVDIM,), jnp.float32), A_log=jnp.log(jax.random.uniform(ks[3], (NHEADS,), jnp.float32, 1.0, 16.0)), D=jnp.ones((NHEADS,), jnp.float32), dt_bias=jax.random.uniform(ks[4], (NHEADS,), jnp.float32, -2.0, 0.0), rms_w=jnp.ones((DINNER,), jnp.float32), out_proj_w=jax.random.normal(ks[5], (DIM, DINNER), jnp.float32) * 0.02)
    _L0_conv_all = _L0_conv_setup()
    _L0_conv_in = {k: v for k, v in _L0_conv_all.items() if k in ('ln_w', 'ln_b', 'in_proj_w', 'conv_w', 'conv_b', 'A_log', 'D', 'dt_bias', 'rms_w', 'out_proj_w', )}
    del _L0_conv_all

    return {
        "x": x,
        "L0_conv_ln_w": _L0_conv_in["ln_w"],
        "L0_conv_ln_b": _L0_conv_in["ln_b"],
        "L0_conv_in_proj_w": _L0_conv_in["in_proj_w"],
        "L0_conv_conv_w": _L0_conv_in["conv_w"],
        "L0_conv_conv_b": _L0_conv_in["conv_b"],
        "L0_conv_A_log": _L0_conv_in["A_log"],
        "L0_conv_D": _L0_conv_in["D"],
        "L0_conv_dt_bias": _L0_conv_in["dt_bias"],
        "L0_conv_rms_w": _L0_conv_in["rms_w"],
        "L0_conv_out_proj_w": _L0_conv_in["out_proj_w"],
    }

def reference(x, L0_conv_ln_w, L0_conv_ln_b, L0_conv_in_proj_w, L0_conv_conv_w, L0_conv_conv_b, L0_conv_A_log, L0_conv_D, L0_conv_dt_bias, L0_conv_rms_w, L0_conv_out_proj_w):
    import jax
    import jax.numpy as jnp
    def _L0_conv_ref(x, ln_w, ln_b, in_proj_w, conv_w, conv_b, A_log, D, dt_bias, rms_w, out_proj_w):
        import jax, jax.numpy as jnp
        import numpy as np
        DIM = 256
        DSTATE = 64
        DCONV = 3
        HEADDIM = 64
        CHUNK = 256
        NGROUPS = 1
        DINNER = int(2.0 * DIM)
        NHEADS = DINNER // HEADDIM
        CONVDIM = DINNER + 2 * NGROUPS * DSTATE
        DPROJ = 2 * DINNER + 2 * NGROUPS * DSTATE + NHEADS

        def _ssd(X, dA, Bm, Cm, chunk):
            b, l, h, p = X.shape
            n = Bm.shape[-1]
            c = l // chunk
            q = chunk
            Xc = X.reshape(b, c, q, h, p)
            Bc = Bm.reshape(b, c, q, h, n)
            Cc = Cm.reshape(b, c, q, h, n)
            Ac = dA.reshape(b, c, q, h).transpose(0, 3, 1, 2)
            Acs = jnp.cumsum(Ac, axis=-1)
            tri = jnp.tril(jnp.ones((q, q), bool))
            Ldec = jnp.where(tri, jnp.exp(Acs[..., :, None] - Acs[..., None, :]), 0.0)
            Y_diag = jnp.einsum('bcqhn,bcshn,bhcqs,bcshp->bcqhp', Cc, Bc, Ldec, Xc)
            decay_states = jnp.exp(Acs[..., -1:] - Acs)
            states = jnp.einsum('bcqhn,bhcq,bcqhp->bchpn', Bc, decay_states, Xc)
            A_last = jnp.pad(Acs[..., -1], ((0, 0), (0, 0), (1, 0)))
            ccs = jnp.cumsum(A_last, axis=-1)
            tric = jnp.tril(jnp.ones((c + 1, c + 1), bool))
            decay_chunk = jnp.where(tric, jnp.exp(ccs[..., :, None] - ccs[..., None, :]), 0.0)
            states0 = jnp.concatenate([jnp.zeros_like(states[:, :1]), states], axis=1)
            prev = jnp.einsum('bhzc,bchpn->bzhpn', decay_chunk, states0)[:, :-1]
            Y_off = jnp.einsum('bcqhn,bchpn,bhcq->bcqhp', Cc, prev, jnp.exp(Acs))
            return (Y_diag + Y_off).reshape(b, l, h, p)

        def _forward(x, ln_w, ln_b, in_proj_w, conv_w, conv_b, A_log, D, dt_bias, rms_w, out_proj_w):
            Bn, Cd, Hh, Ww = x.shape
            L = Hh * Ww
            mu = jnp.mean(x, axis=1, keepdims=True)
            var = jnp.mean((x - mu) ** 2, axis=1, keepdims=True)
            xn = (x - mu) * jax.lax.rsqrt(var + 1e-05)
            xn = xn * ln_w[None, :, None, None] + ln_b[None, :, None, None]
            zxbcdt = jnp.einsum('bchw,dc->bdhw', xn, in_proj_w)
            z = zxbcdt[:, :DINNER]
            xBC = zxbcdt[:, DINNER:DINNER + CONVDIM]
            dt = zxbcdt[:, DINNER + CONVDIM:]
            xBC = jax.lax.conv_general_dilated(xBC, conv_w, (1, 1), 'SAME', dimension_numbers=('NCHW', 'OIHW', 'NCHW'), feature_group_count=CONVDIM)
            xBC = jax.nn.silu(xBC + conv_b[None, :, None, None])

            def to_seq(t):
                return t.reshape(Bn, t.shape[1], L).transpose(0, 2, 1)
            xBC, dt, z = (to_seq(xBC), to_seq(dt), to_seq(z))
            xs = xBC[..., :DINNER].reshape(Bn, L, NHEADS, HEADDIM)
            Bg = xBC[..., DINNER:DINNER + NGROUPS * DSTATE].reshape(Bn, L, NGROUPS, DSTATE)
            Cg = xBC[..., DINNER + NGROUPS * DSTATE:].reshape(Bn, L, NGROUPS, DSTATE)
            hpg = NHEADS // NGROUPS
            Bm = jnp.repeat(Bg, hpg, axis=2)
            Cm = jnp.repeat(Cg, hpg, axis=2)
            dt = jax.nn.softplus(dt + dt_bias[None, None, :])
            A = -jnp.exp(A_log)
            y = _ssd(xs * dt[..., None], dt * A[None, None, :], Bm, Cm, CHUNK)
            y = y + D[None, None, :, None] * xs
            y = y.reshape(Bn, L, DINNER)
            y = y * jax.nn.silu(z)
            y = y * jax.lax.rsqrt(jnp.mean(y * y, axis=-1, keepdims=True) + 1e-05) * rms_w
            out = jnp.einsum('bld,cd->blc', y, out_proj_w)
            out = out.transpose(0, 2, 1).reshape(Bn, Cd, Hh, Ww)
            return x + out
        return _forward(x, ln_w, ln_b, in_proj_w, conv_w, conv_b, A_log, D, dt_bias, rms_w, out_proj_w)

    def _gn(v, G=32, eps=1e-5):
        B_, C_, H_, W_ = v.shape
        g = v.reshape(B_, G, C_ // G, H_, W_)
        m = jnp.mean(g, axis=(2, 3, 4), keepdims=True)
        s = jnp.var(g, axis=(2, 3, 4), keepdims=True)
        return ((g - m) / jnp.sqrt(s + eps)).reshape(v.shape)

    def _ln_c(v, eps=1e-6):
        m = jnp.mean(v, axis=1, keepdims=True)
        s = jnp.var(v, axis=1, keepdims=True)
        return (v - m) / jnp.sqrt(s + eps)

    def _ln_t(v, eps=1e-5):
        m = jnp.mean(v, axis=-1, keepdims=True)
        s = jnp.var(v, axis=-1, keepdims=True)
        return (v - m) / jnp.sqrt(s + eps)

    def _to_tokens(v):
        B_, C_, H_, W_ = v.shape
        return v.reshape(B_, C_, H_ * W_).transpose(0, 2, 1)
    def _from_tokens(t, like):
        B_, C_, H_, W_ = like.shape
        return t.transpose(0, 2, 1).reshape(B_, C_, H_, W_)

    x = _L0_conv_ref(x, L0_conv_ln_w, L0_conv_ln_b, L0_conv_in_proj_w, L0_conv_conv_w, L0_conv_conv_b, L0_conv_A_log, L0_conv_D, L0_conv_dt_bias, L0_conv_rms_w, L0_conv_out_proj_w)
    return x


_drawn_inputs = setup_inputs


def setup_inputs(seed=0):
    import zlib

    import numpy as np

    out = dict(_drawn_inputs(seed))
    spreads = {'L0_conv_ln_w': (1.0, 0.2),
     'L0_conv_ln_b': (0.0, 0.1),
     'L0_conv_conv_b': (0.0, 0.1),
     'L0_conv_D': (1.0, 0.2),
     'L0_conv_rms_w': (1.0, 0.2)}
    factors = {}
    for name, (base, spread) in spreads.items():
        noise = np.random.default_rng([zlib.crc32(name.encode()), seed]).standard_normal(out[name].shape)
        drawn = base * np.exp(spread * noise) if base else spread * noise
        out[name] = jnp.asarray(drawn.astype(out[name].dtype))
    for name, factor in factors.items():
        out[name] = (out[name] * factor).astype(out[name].dtype)
    return out
```

```python
import numpy as np

from concourse import mybir
from concourse.alu_op_type import AluOpType as ALU

F32 = mybir.dt.float32
ACT = mybir.ActivationFunctionType

P = 128
B, DIM, IMG = 8, 256, 64
DINNER, DSTATE, HEADS = 512, 64, 8
HD = DINNER // HEADS
KT = DIM // P
UT = (DINNER + 2 * DSTATE) // P
XT = DINNER // P
DPROJ = 2 * DINNER + 2 * DSTATE + HEADS
ROWS = 8
TOK = ROWS * IMG
CH = TOK // P
GPB = IMG // ROWS
GROUPS = B * GPB
PAD = IMG + 2
EPS = 1e-5
TAPS = 9
PER = dict(
    mean_done=1, var_done=1, u_done=UT, z_done=CH, dt_done=1, decay_done=1, xt_done=CH, gb_done=CH, d_done=CH,
    ydiag_done=CH, yoff_done=CH, state_done=CH, yt_done=CH, o_done=2,
    centered=1, z_biased=CH, dt_biased=1, dt_ready=1, da_ready=1, xdt_ready=CH, dx_ready=CH, gm_ready=CH,
    btok_ready=CH, yoff_scaled=CH, m_ready=CH, y_summed=CH, yn_ready=CH, s_ready=CH, out_ready=2,
    conv_step=TAPS * UT,
    xn_ready=1, r_ready=CH, yd_added=CH, xd_ready=CH, s_decayed=CH, y_gated=CH,
    squared=1, lnvar=1, rstd_ready=1, u_ready=UT, top_halo=1, bottom_halo=UT, dt_abs=1, dt_exp=1, dt_log=1,
    dec_ready=1, e_ready=CH, ss_ready=CH, rms_log=CH, rms_ready=CH, ynt_ready=CH, z_ready=CH, conv_ready=UT + 1,
)


class At:

    def __init__(self, j, i):
        self.j, self.i = j, i

    def __add__(self, k):
        return At(self.j + k, self.i)

    def __sub__(self, k):
        return At(self.j - k, self.i)

    @property
    def known(self):
        return self.j + GPB * self.i if isinstance(self.i, int) else None

    @property
    def exists(self):
        return self.known is None or 0 <= self.known < GROUPS


J0 = 5
LOOPS = (GROUPS - GPB) // GPB
LAST = GROUPS + 2


def steps(eng, body):
    for j in range(-1, J0):
        body(At(j, 0))
    with eng.Fori(0, LOOPS) as i:
        for j in range(J0, J0 + GPB):
            body(At(j, i))
    for j in range(J0, J0 + LAST - (J0 + GPB * LOOPS) + 1):
        body(At(j, LOOPS))


def build(nc, x, w_in, ln_w, ln_b, conv_w, conv_b, conv_bc, a_log, d_skip, dt_bias, rms_w, w_out, out):
    from contextlib import ExitStack

    with ExitStack() as ctx:
        def sb(name, shape, dt=F32):
            return ctx.enter_context(nc.sbuf_tensor(name, [P, *shape], dt))

        sem = {k: ctx.enter_context(nc.semaphore(k)) for k in PER}
        dma = {k: [ctx.enter_context(nc.semaphore(f"{k}{r}")) for r in range(2)]
               for k in ("x_loaded", "xr_loaded", "out_stored")}
        w_loaded = ctx.enter_context(nc.semaphore("w_loaded"))
        const_ready = ctx.enter_context(nc.semaphore("const_ready"))
        w_scaled = ctx.enter_context(nc.semaphore("w_scaled"))
        bias_done = ctx.enter_context(nc.semaphore("bias_done"))
        bias_ready = ctx.enter_context(nc.semaphore("bias_ready"))
        a_exp = ctx.enter_context(nc.semaphore("a_exp"))

        def bank(name, n=1):
            return ctx.enter_context(nc.psum_tensor(name, [P, n, 512], F32))

        big = bank("big", 2)
        dps = bank("dps", 2)
        tps = bank("tps")
        ydps = bank("ydps")
        yops = bank("yops")
        sm = bank("sm")

        w_sb = sb("w_sb", [KT, DPROJ])
        wo_sb = sb("wo_sb", [XT, DIM])
        lnw_sb, lnb_sb = sb("lnw_sb", [KT]), sb("lnb_sb", [KT])
        lnb_bc = sb("lnb_bc", [KT, P])
        cw_sb, cb_sb = sb("cw_sb", [UT, TAPS]), sb("cb_sb", [UT])
        cbc_sb = sb("cbc_sb", [1])
        rms_sb = sb("rms_sb", [XT])
        alog_sb, a_sb, dsk_sb, dtb_sb = (sb(n, [HEADS]) for n in ("alog_sb", "a_sb", "dsk_sb", "dtb_sb"))
        ubias, zbias, dtbias = sb("ubias", [UT]), sb("zbias", [DINNER]), sb("dtbias", [HEADS])
        mean_w, ones, ident, tri, after = (sb(n, [P]) for n in ("mean_w", "ones", "ident", "tri", "after"))
        zeros = sb("zeros", [512])

        xb, xr = sb("xb", [2, KT, TOK]), sb("xr", [2, KT, TOK])
        xc, sq, rstd = sb("xc", [KT, TOK]), sb("sq", [KT, TOK]), sb("rstd", [2, TOK])
        xn = sb("xn", [4, KT, TOK])
        u = sb("u", [2, UT, ROWS + 2, PAD])
        acc = sb("acc", [UT, ROWS, IMG])
        xs = sb("xs", [2, XT, TOK])
        bt, ct = sb("bt", [2, TOK]), sb("ct", [2, TOK])
        z = sb("z", [2, CH, DINNER])
        dtv, dta, dt, da = (sb(n, [k, CH, HEADS]) for n, k in (("dtv", 4), ("dta", 4), ("dt", 4), ("da", 4)))
        dec = sb("dec", [4, 3, CH, HEADS])
        rr = sb("rr", [2, HEADS, P])
        em = sb("em", [2, HEADS, P])
        gm = sb("gm", [2, P])
        btok = sb("btok", [2, DSTATE])
        xdt, xd, dx = sb("xdt", [2, DINNER]), sb("xd", [2, DINNER]), sb("dx", [2, DINNER])
        yb = sb("yb", [2, DINNER])
        junk = sb("junk", [2, DINNER])
        rms = sb("rms", [2, 3])
        ynt = sb("ynt", [XT, TOK])
        st, sd = sb("st", [2, DINNER]), sb("sd", [DINNER])
        ob = sb("ob", [2, KT, TOK])

        block = ctx.enter_context(nc.Block())

        def need(eng, name, n, k=None):
            per = PER[name]
            k = per - 1 if k is None else k
            if n.known is not None:
                if n.known >= 0:
                    eng.wait_ge(sem[name], n.known * per + k + 1)
            else:
                assert n.j >= 0, (name, n.j)
                eng.wait_ge(sem[name], n.i * (GPB * per) + (n.j * per + k + 1))

        def need_dma(eng, name, n):
            count = 16 * (n.j // 2 + 1)
            if n.known is None or n.known >= 0:
                eng.wait_ge(dma[name][n.j % 2], n.i * (GPB // 2 * 16) + count)

        def chunk(n, c):
            return (n + c // CH, c % CH)

        def needc(eng, name, n, c):
            m, k = chunk(n, c)
            need(eng, name, m, k)

        def par(n, c):
            m, k = chunk(n, c)
            return (m.j * CH + k) % 2

        def heads(ap, w=HD):
            return ap.rearrange("p (h d) -> p h d", h=HEADS)

        def per_head(ap, w=HD, rows=P):
            return ap.unsqueeze(2).to_broadcast([rows, HEADS, w])

        BIG = [("mean", 1, 0, "centered"), ("u", 0, 0, "u_ready"), ("u", 0, 1, "u_ready"), ("u", 0, 2, "u_ready"),
               ("u", 0, 3, "u_ready"), ("o", -3, 0, "out_ready"), ("o", -3, 1, "out_ready"),
               ("u", 0, 4, "u_ready"), ("z", -1, 0, "z_biased"), ("var", 1, 0, "lnvar"), ("z", -1, 1, "z_biased"),
               ("z", -1, 2, "z_biased"), ("z", -1, 3, "z_biased")]
        NBIG = len(BIG)
        where = {(b[0], b[2]): q for q, b in enumerate(BIG)}

        def big_bank(t, what, part=0):
            return (t.j * NBIG + where[what, part]) % 2

        def big_free(eng, t, what, part=0):
            q = where[what, part] - 2
            s = t + (q // NBIG)
            kind, d, k, free = BIG[q % NBIG]
            if (s + d).exists:
                need(eng, free, s + d, k)
            else:
                while (q // NBIG + t.known) >= -1:
                    q -= 2
                    s = t + (q // NBIG)
                    kind, d, k, free = BIG[q % NBIG]
                    if (s + d).exists:
                        need(eng, free, s + d, k)
                        return

        def convolve(eng, t, lo, hi):
            n = t - 1
            if not n.exists:
                return
            for q in range(lo, hi):
                tap, m = divmod(q, UT)
                dy, dx_ = divmod(tap, 3)
                if q == 0:
                    need(eng, "top_halo", n)
                    need(eng, "u_ready", n)
                    need(eng, "conv_ready", n - 1)
                if dy == 2 and dx_ == 0:
                    need(eng, "bottom_halo", n + 1, m)
                src = u[:, n.j % 2, m, dy:dy + ROWS, dx_:dx_ + IMG]
                w = cw_sb[:, m, tap:tap + 1]
                if tap:
                    need(eng, "conv_step", n, q - UT)
                other = acc[:, m] if tap else zeros[:].rearrange("p (r w) -> p r w", r=ROWS)
                eng.scalar_tensor_tensor(acc[:, m], src, w, other, ALU.mult, ALU.add).then_inc(
                    sem["conv_step"], 1)

        @block.sync
        def _(sp):
            for dst, src in ((w_sb, w_in), (wo_sb, w_out), (lnw_sb, ln_w), (lnb_sb, ln_b), (cw_sb, conv_w),
                             (cb_sb, conv_b), (rms_sb, rms_w), (alog_sb, a_log), (dsk_sb, d_skip),
                             (dtb_sb, dt_bias)):
                sp.dma_start(dst[:], src).then_inc(w_loaded, 16)
            sp.dma_start(cbc_sb[0:DSTATE, :], conv_bc).then_inc(w_loaded, 16)

            def image(dram, n):
                g = n.j % GPB
                return dram[n.i + n.j // GPB, :, :, g * TOK:(g + 1) * TOK]

            def load(n):
                if n.exists:
                    need(sp, "centered", n - 2)
                    sp.dma_start(xb[:, n.j % 2], image(x, n)).then_inc(dma["x_loaded"][n.j % 2], 16)

            def step(t):
                if t.known == -1:
                    load(t + 1)
                load(t + 2)
                n = t - 2
                if n.exists:
                    need(sp, "out_ready", n - 2)
                    sp.dma_start(xr[:, n.j % 2], image(x, n)).then_inc(dma["xr_loaded"][n.j % 2], 16)
                n = t - 3
                if n.exists:
                    need(sp, "out_ready", n)
                    sp.dma_start(image(out, n), ob[:, n.j % 2]).then_inc(dma["out_stored"][n.j % 2], 16)

            steps(sp, step)
            for stored in dma["out_stored"]:
                sp.wait_ge(stored, GROUPS // 2 * 16)

        @block.tensor
        def _(pe):
            pe.wait_ge(const_ready, 10)
            pe.wait_ge(w_loaded, 16 * 11)
            for m in range(UT):
                for k in range(KT):
                    last = pe.matmul(sm[:, 0, m:m + 1], w_sb[:, k, DINNER + m * P:DINNER + (m + 1) * P],
                                     lnb_sb[:, k:k + 1], start=k == 0, stop=k == KT - 1)
            last.then_inc(bias_done, 1)
            pe.wait_ge(w_scaled, 1)
            for lo, w, dst in ((0, DINNER, ydps[:, 0, :]), (DPROJ - HEADS, HEADS, yops[:, 0, 0:HEADS])):
                for k in range(KT):
                    last = pe.matmul(dst, lnb_bc[:, k, :], w_sb[:, k, lo:lo + w], start=k == 0, stop=k == KT - 1)
            last.then_inc(bias_done, 1)
            pe.wait_ge(w_scaled, 4)

            def mean(t):
                n = t + 1
                if n.exists:
                    need_dma(pe, "x_loaded", n)
                    big_free(pe, t, "mean")
                    for k in range(KT):
                        last = pe.matmul(big[:, big_bank(t, "mean"), :], mean_w[:], xb[:, n.j % 2, k, :],
                                         start=k == 0, stop=k == KT - 1)
                    last.then_inc(sem["mean_done"], 1)

            def var(t):
                n = t + 1
                if n.exists:
                    need(pe, "squared", n)
                    big_free(pe, t, "var")
                    for k in range(KT):
                        last = pe.matmul(big[:, big_bank(t, "var"), :], mean_w[:], sq[:, k, :],
                                         start=k == 0, stop=k == KT - 1)
                    last.then_inc(sem["var_done"], 1)

            def project_u(t, m):
                if t.exists:
                    if m == 0:
                        need(pe, "xn_ready", t)
                    big_free(pe, t, "u", m)
                    for k in range(KT):
                        last = pe.matmul(big[:, big_bank(t, "u", m), :],
                                         w_sb[:, k, DINNER + m * P:DINNER + (m + 1) * P], xn[:, t.j % 4, k, :],
                                         start=k == 0, stop=k == KT - 1)
                    last.then_inc(sem["u_done"], 1)

            def project_z(t, c):
                n = t - 1
                if n.exists:
                    big_free(pe, t, "z", c)
                    for k in range(KT):
                        last = pe.matmul(big[:, big_bank(t, "z", c), :], xn[:, n.j % 4, k, c * P:(c + 1) * P],
                                         w_sb[:, k, 0:DINNER], start=k == 0, stop=k == KT - 1)
                    last.then_inc(sem["z_done"], 1)

            def project_dt(t):
                if t.exists:
                    need(pe, "btok_ready", t - 2)
                    if t.known is not None and 0 < t.known < 2:
                        need(pe, "dec_ready", t - 1)
                    for c in range(CH):
                        for k in range(KT):
                            last = pe.matmul(sm[:, 0, c * HEADS:(c + 1) * HEADS],
                                             xn[:, t.j % 4, k, c * P:(c + 1) * P], w_sb[:, k, DPROJ - HEADS:],
                                             start=k == 0, stop=k == KT - 1)
                    last.then_inc(sem["dt_done"], 1)

            def decays(t):
                n = t - 1
                if n.exists:
                    need(pe, "da_ready", n)
                    if (t - 2).exists:
                        need(pe, "btok_ready", t - 2, 0)
                    else:
                        need(pe, "dt_biased", n)
                    for k, w in enumerate((tri, after, ones)):
                        last = pe.matmul(sm[:, 0, 32 * k:32 * k + 32], w[:],
                                         da[:, n.j % 4].rearrange("p c h -> p (c h)"), start=True, stop=True)
                    last.then_inc(sem["decay_done"], 1)

            def project_out(t, m):
                n = t - 3
                if n.exists:
                    if m == 0:
                        need(pe, "ynt_ready", n)
                    big_free(pe, t, "o", m)
                    for k in range(XT):
                        last = pe.matmul(big[:, big_bank(t, "o", m), :], wo_sb[:, k, m * P:(m + 1) * P],
                                         ynt[:, k, :], start=k == 0, stop=k == XT - 1)
                    last.then_inc(sem["o_done"], 1)

            def first(t, c):
                n = t - 2
                if not n.exists:
                    return
                tok = slice(c * P, (c + 1) * P)
                if c == 0:
                    need(pe, "conv_ready", n)
                needc(pe, "ynt_ready", n, c - 3)
                for k in range(XT):
                    last = pe.transpose(tps[:, 0, k * P:(k + 1) * P], xs[:, n.j % 2, k, tok], ident[:])
                last.then_inc(sem["xt_done"], 1)
                needc(pe, "e_ready", n, c - 1)
                need(pe, "r_ready", n, c)
                for k in range(2):
                    last = pe.matmul(dps[:, k, :], after[:],
                                     rr[:, c % 2, 4 * k:4 * k + 4, :].rearrange("p h q -> p (h q)"),
                                     start=True, stop=True)
                last.then_inc(sem["d_done"], 1)
                if c <= 1:
                    need(pe, ("dt_biased", "dec_ready")[c], n + 1 if (n + 1).exists else n)
                if c or n.known == GROUPS - 1:
                    needc(pe, "btok_ready", n, c - 1)
                pe.matmul(sm[:, 0, 0:P], bt[0:DSTATE, n.j % 2, tok], ct[0:DSTATE, n.j % 2, tok],
                          start=True, stop=True)
                pe.transpose(sm[:, 0, P:P + DSTATE], bt[0:DSTATE, n.j % 2, tok],
                             ident[0:DSTATE, 0:DSTATE]).then_inc(sem["gb_done"], 1)

            def off(t, c):
                n, k = chunk(t - 2, c - 1)
                if not n.exists:
                    return
                start = n.j % GPB == 0 and k == 0
                needc(pe, "s_ready", n, k - 1)
                s = zeros if start else st[:, (k - 1) % 2]
                pe.matmul(yops[:, 0, :], ct[0:DSTATE, n.j % 2, k * P:(k + 1) * P], s[0:DSTATE, :],
                          start=True, stop=True).then_inc(sem["yoff_done"], 1)

            def diag(t, c):
                n, k = chunk(t - 2, c - 1)
                if not n.exists:
                    return
                need(pe, "m_ready", n, k)
                needc(pe, "y_summed", n, k - 1)
                for h in range(HEADS):
                    last = pe.matmul(ydps[:, 0, h * HD:(h + 1) * HD], em[:, k % 2, h, :],
                                     xdt[:, k % 2, h * HD:(h + 1) * HD], start=True, stop=True)
                last.then_inc(sem["ydiag_done"], 1)

            def state(t, c):
                n, k = chunk(t - 2, c - 1)
                if not n.exists:
                    return
                need(pe, "xd_ready", n, k)
                need(pe, "yoff_scaled", n, k)
                pe.matmul(yops[0:DSTATE, 0, :], btok[:, k % 2, :], xd[:, k % 2, :],
                          start=True, stop=True).then_inc(sem["state_done"], 1)

            def turn(t, c):
                n, k = chunk(t - 2, c - 2)
                if not n.exists:
                    return
                need(pe, "yn_ready", n, k)
                m, q = chunk(t - 2, c)
                if m.exists:
                    need(pe, "dx_ready", m, q)
                elif n.exists:
                    need(pe, "ynt_ready", *chunk(n, k - 1))
                for j in range(XT):
                    last = pe.transpose(tps[:, 0, j * P:(j + 1) * P], yb[:, k % 2, j * P:(j + 1) * P], ident[:])
                last.then_inc(sem["yt_done"], 1)

            def step(t):
                for c in range(CH):
                    if c == 0:
                        mean(t)
                    if c == 1:
                        decays(t)
                    first(t, c)
                    off(t, c)
                    if c == 0:
                        project_u(t, 0)
                        project_u(t, 1)
                    if c == 1:
                        project_u(t, 2)
                        project_u(t, 3)
                    if c == 2:
                        project_u(t, 4)
                    if c == 3:
                        project_z(t, 1)
                    diag(t, c)
                    turn(t, c)
                    if c == 1:
                        project_out(t, 0)
                        project_out(t, 1)
                    if c == 2:
                        project_z(t, 0)
                        var(t)
                    if c == 3:
                        project_z(t, 2)
                        project_z(t, 3)
                        project_dt(t)
                    state(t, c)

            steps(pe, step)

        @block.scalar
        def _(act):
            act.wait_ge(w_loaded, 16 * 11)
            act.activation(a_sb[:], alog_sb[:], ACT.Exp).then_inc(a_exp, 1)
            act.wait_ge(const_ready, 10)

            def square(t):
                n = t + 1
                if n.exists:
                    need(act, "centered", n)
                    need(act, "var_done", n - 1)
                    act.activation(sq[:], xc[:], ACT.Square).then_inc(sem["squared"], 1)

            def rstd_of(t):
                n = t + 1
                if n.exists:
                    need(act, "var_done", n)
                    act.activation(rstd[:, 0, :], big[:, big_bank(t, "var"), :], ACT.Ln, bias=EPS).then_inc(
                        sem["lnvar"], 1)
                    need(act, "lnvar", n)
                    need(act, "xn_ready", n - 1)
                    act.activation(rstd[:, 1, :], rstd[:, 0, :], ACT.Exp, scale=-0.5).then_inc(sem["rstd_ready"], 1)

            def top(t):
                n = t
                if n.exists:
                    need(act, "conv_step", n - 2)
                    need(act, "u_ready", n - 1)
                    dst = u[:, n.j % 2, :, 0, 1:IMG + 1]
                    if n.j % GPB == 0:
                        src = zeros[:, 0:UT * IMG].rearrange("p (m w) -> p m w", m=UT)
                    else:
                        src = u[:, (n.j - 1) % 2, :, ROWS, 1:IMG + 1]
                    act.activation(dst, src, ACT.Copy).then_inc(sem["top_halo"], 1)

            def u_rows(t, m):
                n = t
                if n.exists:
                    need(act, "u_done", n, m)
                if (n - 1).exists:
                    dst = u[:, (n.j - 1) % 2, m, ROWS + 1, 1:IMG + 1]
                    if n.j % GPB == 0:
                        i = act.activation(dst, zeros[:, 0:IMG], ACT.Copy)
                    else:
                        i = act.activation(dst, big[:, big_bank(t, "u", m), 0:IMG], ACT.Identity,
                                           bias=ubias[:, m:m + 1])
                    i.then_inc(sem["bottom_halo"], 1)
                elif n.known == 0:
                    act.activation(junk[:, 0, 0:IMG], zeros[:, 0:IMG], ACT.Copy).then_inc(sem["bottom_halo"], 1)
                    if m < UT - 1:
                        need(act, "bottom_halo", n, m)
                if n.exists:
                    act.activation(u[:, n.j % 2, m, 1:ROWS + 1, 1:IMG + 1],
                                   big[:, big_bank(t, "u", m), :].rearrange("p (r w) -> p r w", r=ROWS),
                                   ACT.Identity, bias=ubias[:, m:m + 1]).then_inc(sem["u_ready"], 1)

            def softplus(t):
                n = t
                if n.exists:
                    need(act, "dt_biased", n)
                    v, a = dtv[:, n.j % 4], dta[:, n.j % 4]
                    act.activation(a, v, ACT.Abs).then_inc(sem["dt_abs"], 1)
                    need(act, "dt_abs", n)
                    act.activation(a, a, ACT.Exp, scale=-1.0).then_inc(sem["dt_exp"], 1)
                    need(act, "dt_exp", n)
                    act.activation(a, a, ACT.Ln, bias=1.0).then_inc(sem["dt_log"], 1)

            def decays(t):
                n = t - 1
                if n.exists:
                    need(act, "decay_done", n)
                    act.activation(dec[:, n.j % 4].rearrange("p k c h -> p (k c h)"), sm[:, 0, 0:96],
                                   ACT.Exp).then_inc(sem["dec_ready"], 1)

            def exps(t, c):
                n = t - 2
                if n.exists:
                    need(act, "d_done", n, c)
                    needc(act, "ydiag_done", n, c - 2)
                    act.activation(em[:, c % 2].rearrange("p h q -> p (h q)"),
                                   dps[:].rearrange("p k q -> p (k q)"), ACT.Exp).then_inc(sem["e_ready"], 1)

            def rms_of(t, c):
                n, k = chunk(t - 2, c - 1)
                if n.exists:
                    need(act, "y_gated", n, k)
                    needc(act, "yn_ready", n, k - 2)
                    act.activation(junk[:, k % 2, :], yb[:, k % 2, :], ACT.Square,
                                   accum_out=rms[:, k % 2, 0:1]).then_inc(sem["ss_ready"], 1)
                    need(act, "ss_ready", n, k)
                    act.activation(rms[:, k % 2, 1:2], rms[:, k % 2, 0:1], ACT.Ln, bias=EPS,
                                   scale=1.0 / DINNER).then_inc(sem["rms_log"], 1)
                    need(act, "rms_log", n, k)
                    act.activation(rms[:, k % 2, 2:3], rms[:, k % 2, 1:2], ACT.Exp, scale=-0.5).then_inc(
                        sem["rms_ready"], 1)

            def turned(t, c):
                n, k = chunk(t - 2, c - 2)
                if n.exists:
                    need(act, "yt_done", n, k)
                    if k == 0:
                        need(act, "o_done", n - 1)
                    act.activation(ynt[:, :, k * P:(k + 1) * P],
                                   tps[:, 0, :].rearrange("p (j q) -> p j q", j=XT),
                                   ACT.Copy).then_inc(sem["ynt_ready"], 1)

            def silu_conv(t):
                n = t - 1
                if not n.exists:
                    return
                need(act, "conv_step", n)
                need(act, "yoff_done", n - 2)
                for m in range(XT):
                    act.activation(xs[:, n.j % 2, m, :], acc[:, m].rearrange("p r w -> p (r w)"), ACT.Silu,
                                   bias=cb_sb[:, m:m + 1]).then_inc(sem["conv_ready"], 1)
                for dst, rows, bias in ((bt, slice(0, DSTATE), cb_sb[0:DSTATE, XT:UT]),
                                        (ct, slice(DSTATE, P), cb_sb[DSTATE:P, XT:UT])):
                    act.activation(dst[0:DSTATE, n.j % 2, :], acc[rows, XT].rearrange("p r w -> p (r w)"),
                                   ACT.Silu, bias=cbc_sb[0:DSTATE, :] if dst is ct else bias).then_inc(
                                       sem["conv_ready"], 1)

            def silu_z(t, c):
                n = t - 1
                if n.exists:
                    need(act, "z_biased", n, c)
                    act.activation(z[:, n.j % 2, c, :], z[:, n.j % 2, c, :], ACT.Silu).then_inc(sem["z_ready"], 1)

            def step(t):
                for c in range(CH):
                    if c == 0:
                        softplus(t - 1)
                    if c == 1:
                        decays(t)
                    exps(t, c)
                    if c == 0:
                        top(t)
                        u_rows(t, 0)
                        u_rows(t, 1)
                        square(t)
                    if c == 1:
                        u_rows(t, 2)
                        u_rows(t, 3)
                    if c == 2:
                        u_rows(t, 4)
                    turned(t, c)
                    rms_of(t, c)
                    if c == 2:
                        rstd_of(t)
                for c in range(CH):
                    silu_z(t, c)
                silu_conv(t)

            steps(act, step)

        @block.vector
        def _(dve):
            dve.wait_ge(w_loaded, 16 * 11)
            for k in range(KT):
                i = dve.tensor_copy(lnb_bc[:, k, :], lnb_sb[:, k:k + 1].to_broadcast([P, P]))
            i.then_inc(w_scaled, 1)
            dve.wait_ge(bias_done, 2)
            for k in range(KT):
                i = dve.tensor_scalar(w_sb[:, k, :], w_sb[:, k, :], lnw_sb[:, k:k + 1], None, ALU.mult)
            i.then_inc(w_scaled, 1)
            for k in range(XT):
                i = dve.tensor_scalar(wo_sb[:, k, :], wo_sb[:, k, :], rms_sb[:, k:k + 1], None, ALU.mult)
            i.then_inc(w_scaled, 1)
            dve.tensor_copy(ubias[:], sm[:, 0, 0:UT]).then_inc(bias_ready, 1)
            dve.tensor_copy(zbias[:], ydps[:, 0, :]).then_inc(bias_ready, 1)
            dve.tensor_tensor(dtbias[:], dtb_sb[:], yops[:, 0, 0:HEADS], ALU.add).then_inc(bias_ready, 1)
            dve.wait_ge(a_exp, 1)
            dve.tensor_scalar(a_sb[:], a_sb[:], -1.0, None, ALU.mult).then_inc(bias_ready, 1)
            dve.wait_ge(bias_ready, 4)
            dve.nop().then_inc(w_scaled, 1)
            dve.wait_ge(const_ready, 10)

            def center(t):
                n = t + 1
                if n.exists:
                    need(dve, "mean_done", n)
                    need(dve, "xn_ready", n - 1)
                    dve.tensor_tensor(xc[:], xb[:, n.j % 2],
                                      big[:, big_bank(t, "mean"), :].unsqueeze(1).to_broadcast([P, KT, TOK]),
                                      ALU.subtract).then_inc(sem["centered"], 1)

            def z_bias(t, c):
                n = t - 1
                if n.exists:
                    need(dve, "z_done", n, c)
                    need(dve, "y_gated", n - 2, c)
                    dve.tensor_tensor(z[:, n.j % 2, c, :], big[:, big_bank(t, "z", c), :], zbias[:],
                                      ALU.add).then_inc(sem["z_biased"], 1)

            def dt_bias_add(t):
                n = t
                if n.exists:
                    need(dve, "dt_done", n)
                    dve.tensor_tensor(dtv[:, n.j % 4], sm[:, 0, 0:32].rearrange("p (c h) -> p c h", c=CH),
                                      dtbias[:].unsqueeze(1).to_broadcast([P, CH, HEADS]),
                                      ALU.add).then_inc(sem["dt_biased"], 1)

            def dt_end(t):
                n = t
                if n.exists:
                    need(dve, "dt_log", n)
                    dve.scalar_tensor_tensor(dt[:, n.j % 4], dtv[:, n.j % 4], 0.0, dta[:, n.j % 4],
                                             ALU.max, ALU.add).then_inc(sem["dt_ready"], 1)
                    need(dve, "dt_ready", n)
                    dve.tensor_tensor(da[:, n.j % 4], dt[:, n.j % 4],
                                      a_sb[:].unsqueeze(1).to_broadcast([P, CH, HEADS]),
                                      ALU.mult).then_inc(sem["da_ready"], 1)

            def x_tokens(t, c):
                n = t - 2
                if n.exists:
                    need(dve, "xt_done", n, c)
                    needc(dve, "xd_ready", n, c - 2)
                    needc(dve, "ydiag_done", n, c - 2)
                    dve.tensor_tensor(heads(xdt[:, c % 2, :]), heads(tps[:, 0, :]),
                                      per_head(dt[:, n.j % 4, c, :]), ALU.mult).then_inc(sem["xdt_ready"], 1)
                    needc(dve, "yd_added", n, c - 2)
                    dve.tensor_tensor(heads(dx[:, c % 2, :]), heads(tps[:, 0, :]), per_head(dsk_sb[:]),
                                      ALU.mult).then_inc(sem["dx_ready"], 1)

            def small(t, c):
                n = t - 2
                if n.exists:
                    need(dve, "gb_done", n, c)
                    needc(dve, "m_ready", n, c - 2)
                    dve.tensor_tensor(gm[:, c % 2, :], sm[:, 0, 0:P], tri[:], ALU.mult).then_inc(sem["gm_ready"], 1)
                    needc(dve, "state_done", n, c - 2)
                    dve.tensor_copy(btok[:, c % 2, :], sm[:, 0, P:P + DSTATE]).then_inc(sem["btok_ready"], 1)

            def masked(t, c):
                n = t - 2
                if n.exists:
                    need(dve, "e_ready", n, c)
                    need(dve, "gm_ready", n, c)
                    dve.tensor_tensor(em[:, c % 2], em[:, c % 2],
                                      gm[:, c % 2, :].unsqueeze(1).to_broadcast([P, HEADS, P]),
                                      ALU.mult).then_inc(sem["m_ready"], 1)

            def off_scale(t, c):
                n, k = chunk(t - 2, c - 1)
                if n.exists:
                    need(dve, "yoff_done", n, k)
                    needc(dve, "yt_done", n, k - 2)
                    dve.tensor_tensor(heads(yb[:, k % 2, :]), heads(yops[:, 0, :]),
                                      per_head(dec[:, n.j % 4, 0, k, :]), ALU.mult).then_inc(sem["yoff_scaled"], 1)

            def sum_y(t, c):
                n, k = chunk(t - 2, c - 1)
                if n.exists:
                    need(dve, "ydiag_done", n, k)
                    need(dve, "yd_added", n, k)
                    dve.tensor_tensor(yb[:, k % 2, :], yb[:, k % 2, :], ydps[:, 0, :],
                                      ALU.add).then_inc(sem["y_summed"], 1)

            def new_state(t, c):
                n, k = chunk(t - 2, c - 1)
                if n.exists:
                    need(dve, "state_done", n, k)
                    need(dve, "s_decayed", n, k)
                    dve.tensor_tensor(st[0:DSTATE, k % 2, :], sd[0:DSTATE, :], yops[0:DSTATE, 0, :],
                                      ALU.add).then_inc(sem["s_ready"], 1)

            def normalise(t, c):
                n, k = chunk(t - 2, c - 2)
                if n.exists:
                    need(dve, "rms_ready", n, k)
                    dve.tensor_scalar(yb[:, k % 2, :], yb[:, k % 2, :], rms[:, k % 2, 2:3], None,
                                      ALU.mult).then_inc(sem["yn_ready"], 1)

            def finish(t, m):
                n = t - 3
                if n.exists:
                    need(dve, "o_done", n, m)
                    if m == 0:
                        need_dma(dve, "xr_loaded", n)
                        need_dma(dve, "out_stored", n - 2)
                    dve.tensor_tensor(ob[:, n.j % 2, m, :], xr[:, n.j % 2, m, :],
                                      big[:, big_bank(t, "o", m), :], ALU.add).then_inc(sem["out_ready"], 1)

            def step(t):
                for c in range(CH):
                    if c == 0:
                        dt_end(t - 1)
                        center(t)
                    normalise(t, c)
                    x_tokens(t, c)
                    small(t, c)
                    if c == 3:
                        z_bias(t, 0)
                    off_scale(t, c)
                    convolve(dve, t, *((0, 5), (15, 20), (30, 35), (45, 45))[c])
                    masked(t, c)
                    if c == 3:
                        z_bias(t, 1)
                    sum_y(t, c)
                    convolve(dve, t, *((5, 15), (20, 25), (35, 40), (45, 45))[c])
                    if c == 1:
                        finish(t, 0)
                        finish(t, 1)
                        convolve(dve, t, 25, 30)
                    if c == 2:
                        convolve(dve, t, 40, 45)
                    if c == 3:
                        z_bias(t, 2)
                        z_bias(t, 3)
                        dt_bias_add(t)
                    new_state(t, c)

            steps(dve, step)

        @block.gpsimd
        def _(pool):
            pool.memset(mean_w[:], 1.0 / DIM).then_inc(const_ready, 1)
            pool.memset(ones[:], 1.0).then_inc(const_ready, 1)
            pool.memset(zeros[:], 0.0).then_inc(const_ready, 1)
            pool.memset(u[:], 0.0).then_inc(const_ready, 1)
            for c in (ident, tri, after):
                last = pool.memset(c[:], 1.0)
            last.then_inc(const_ready, 1)
            pool.wait_ge(const_ready, 5)
            pool.affine_select(out=ident[:], in_=ident[:], compare_op=ALU.is_equal, fill=0.0, base=0,
                               pattern=[[-1, P]], channel_multiplier=1).then_inc(const_ready, 1)
            pool.affine_select(out=tri[:], in_=tri[:], compare_op=ALU.is_ge, fill=0.0, base=0,
                               pattern=[[1, P]], channel_multiplier=-1).then_inc(const_ready, 1)
            pool.affine_select(out=after[:], in_=after[:], compare_op=ALU.is_gt, fill=0.0, base=0,
                               pattern=[[-1, P]], channel_multiplier=1).then_inc(const_ready, 1)
            pool.memset(yb[:], 0.0).then_inc(const_ready, 1)
            pool.wait_ge(const_ready, 9)
            pool.memset(junk[:], 0.0).then_inc(const_ready, 1)
            pool.wait_ge(const_ready, 10)
            pool.wait_ge(w_loaded, 16 * 11)

            def product(out_, a, b, name, op=ALU.mult):
                pool.tensor_tensor(out_, a, b, op).then_inc(sem[name], 1)

            def norm(t):
                n = t + 1
                if n.exists:
                    need(pool, "rstd_ready", n)
                    need(pool, "z_done", n - 4)
                    product(xn[:, n.j % 4], xc[:], rstd[:, 1, :].unsqueeze(1).to_broadcast([P, KT, TOK]),
                            "xn_ready")

            def ramps(t, c):
                n, k = chunk(t - 2, c + 1)
                if n.exists:
                    if k == 0:
                        need(pool, "da_ready", n)
                    needc(pool, "d_done", n, k - 2)
                    product(rr[:, k % 2], tri[:].unsqueeze(1).to_broadcast([P, HEADS, P]),
                            per_head(da[:, n.j % 4, k, :], P), "r_ready")

            def skip(t, c):
                n, k = chunk(t - 2, c - 1)
                if n.exists:
                    need(pool, "yoff_scaled", n, k)
                    product(yb[:, k % 2, :], yb[:, k % 2, :], dx[:, k % 2, :], "yd_added", ALU.add)

            def decayed_x(t, c):
                n = t - 2
                if n.exists:
                    need(pool, "xdt_ready", n, c)
                    needc(pool, "state_done", n, c - 2)
                    product(heads(xd[:, c % 2, :]), heads(xdt[:, c % 2, :]), per_head(dec[:, n.j % 4, 1, c, :]),
                            "xd_ready")

            def decayed_state(t, c):
                n, k = chunk(t - 2, c - 1)
                if n.exists:
                    needc(pool, "s_ready", n, k - 1)
                    start = n.j % GPB == 0 and k == 0
                    s = zeros[0:DSTATE, :] if start else st[0:DSTATE, (k - 1) % 2, :]
                    product(heads(sd[0:DSTATE, :]), heads(s), per_head(dec[0:DSTATE, n.j % 4, 2, k, :], rows=DSTATE),
                            "s_decayed")

            def gate(t, c):
                n, k = chunk(t - 2, c - 1)
                if n.exists:
                    need(pool, "y_summed", n, k)
                    need(pool, "z_ready", n, k)
                    product(yb[:, k % 2, :], yb[:, k % 2, :], z[:, n.j % 2, k, :], "y_gated")

            def step(t):
                for c in range(CH):
                    skip(t, c)
                    decayed_state(t, c)
                    decayed_x(t, c)
                    ramps(t, c)
                    gate(t, c)
                norm(t)

            steps(pool, step)


def kernel(x, L0_conv_ln_w, L0_conv_ln_b, L0_conv_in_proj_w, L0_conv_conv_w, L0_conv_conv_b, L0_conv_A_log,
           L0_conv_D, L0_conv_dt_bias, L0_conv_rms_w, L0_conv_out_proj_w):
    import concourse.bacc as bacc
    from concourse.bass_utils import run_bass_kernel_spmd

    def rows(a, n):
        a = np.asarray(a)
        return np.ascontiguousarray(np.moveaxis(a.reshape(n, P, *a.shape[1:]), 0, 1))

    def everywhere(a):
        return np.ascontiguousarray(np.broadcast_to(np.asarray(a), (P, a.shape[0])))

    xv = np.ascontiguousarray(np.asarray(x).reshape(B, KT, P, IMG * IMG).transpose(0, 2, 1, 3))
    arrays = {
        "x": xv,
        "w_in": rows(np.asarray(L0_conv_in_proj_w).T, KT),
        "ln_w": rows(L0_conv_ln_w, KT), "ln_b": rows(L0_conv_ln_b, KT),
        "conv_w": rows(np.asarray(L0_conv_conv_w).reshape(UT * P, TAPS), UT), "conv_b": rows(L0_conv_conv_b, UT),
        "conv_bc": np.ascontiguousarray(np.asarray(L0_conv_conv_b)[-DSTATE:, None]),
        "a_log": everywhere(L0_conv_A_log), "d_skip": everywhere(L0_conv_D),
        "dt_bias": everywhere(L0_conv_dt_bias),
        "rms_w": rows(L0_conv_rms_w, XT), "w_out": rows(np.asarray(L0_conv_out_proj_w).T, XT),
    }
    nc = bacc.Bacc("TRN2", target_bir_lowering=False, num_devices=1)
    args = [nc.dram_tensor(f"in_{k}", a.shape, mybir.dt.from_np(a.dtype), kind="ExternalInput").ap()
            for k, a in arrays.items()]
    out = nc.dram_tensor("out", xv.shape, F32, kind="ExternalOutput").ap()
    build(nc, *args, out)
    r = run_bass_kernel_spmd(nc, [{f"in_{k}": a for k, a in arrays.items()}], core_ids=[0])
    got = r.results[0]["out"]
    return np.ascontiguousarray(got.transpose(0, 2, 1, 3)).reshape(B, DIM, IMG, IMG)
```

```python
import numpy as np

from concourse import mybir
from concourse.alu_op_type import AluOpType as ALU

F32 = mybir.dt.float32
ACT = mybir.ActivationFunctionType

P = 128
B, DIM, IMG = 8, 256, 64
DINNER, DSTATE, HEADS = 512, 64, 8
HD = DINNER // HEADS
KT = DIM // P
UT = (DINNER + 2 * DSTATE) // P
XT = DINNER // P
DPROJ = 2 * DINNER + 2 * DSTATE + HEADS
ROWS = 8
TOK = ROWS * IMG
CH = TOK // P
GPB = IMG // ROWS
GROUPS = B * GPB
PAD = IMG + 2
EPS = 1e-5
TAPS = 9
VT = (0, 1, 2, 3)
AT = (4,)
PER = dict(
    mean_done=1, var_done=1, u_done=UT, z_done=CH, dt_done=1, decay_done=1, xt_done=CH, gb_done=CH, d_done=CH,
    ydiag_done=CH, yoff_done=CH, state_done=CH, yt_done=CH, o_done=2,
    centered=1, z_biased=CH, dt_biased=1, dt_ready=1, da_ready=1, xdt_ready=CH, dx_ready=CH, gm_ready=CH,
    btok_ready=CH, yoff_scaled=CH, m_ready=CH, y_summed=CH, yn_ready=CH, s_ready=CH, out_ready=2,
    conv_step=TAPS * len(VT), tap_made=TAPS * len(AT), tap_added=(TAPS - 1) * len(AT),
    xn_ready=1, r_ready=CH, yd_added=CH, xd_ready=CH, s_decayed=CH, y_gated=CH,
    squared=1, lnvar=1, rstd_ready=1, u_ready=UT, top_halo=1, bottom_halo=UT, dt_abs=1, dt_exp=1, dt_log=1,
    dec_ready=1, e_ready=CH, ss_ready=CH, rms_log=CH, rms_ready=CH, ynt_ready=CH, z_ready=CH, conv_ready=UT + 1,
)


class At:

    def __init__(self, j, i):
        self.j, self.i = j, i

    def __add__(self, k):
        return At(self.j + k, self.i)

    def __sub__(self, k):
        return At(self.j - k, self.i)

    @property
    def known(self):
        return self.j + GPB * self.i if isinstance(self.i, int) else None

    @property
    def exists(self):
        return self.known is None or 0 <= self.known < GROUPS


J0 = 5
LOOPS = (GROUPS - GPB) // GPB
LAST = GROUPS + 2


def steps(eng, body):
    for j in range(-1, J0):
        body(At(j, 0))
    with eng.Fori(0, LOOPS) as i:
        for j in range(J0, J0 + GPB):
            body(At(j, i))
    for j in range(J0, J0 + LAST - (J0 + GPB * LOOPS) + 1):
        body(At(j, LOOPS))


def build(nc, x, w_in, ln_w, ln_b, conv_w, conv_b, conv_bc, a_log, d_skip, dt_bias, rms_w, w_out, out):
    from contextlib import ExitStack

    with ExitStack() as ctx:
        def sb(name, shape, dt=F32):
            return ctx.enter_context(nc.sbuf_tensor(name, [P, *shape], dt))

        sem = {k: ctx.enter_context(nc.semaphore(k)) for k in PER}
        dma = {k: [ctx.enter_context(nc.semaphore(f"{k}{r}")) for r in range(2)]
               for k in ("x_loaded", "xr_loaded", "out_stored")}
        w_loaded = ctx.enter_context(nc.semaphore("w_loaded"))
        const_ready = ctx.enter_context(nc.semaphore("const_ready"))
        w_scaled = ctx.enter_context(nc.semaphore("w_scaled"))
        bias_done = ctx.enter_context(nc.semaphore("bias_done"))
        bias_ready = ctx.enter_context(nc.semaphore("bias_ready"))
        a_exp = ctx.enter_context(nc.semaphore("a_exp"))

        def bank(name, n=1):
            return ctx.enter_context(nc.psum_tensor(name, [P, n, 512], F32))

        big = bank("big", 2)
        dps = bank("dps", 2)
        tps = bank("tps")
        ydps = bank("ydps")
        yops = bank("yops")
        sm = bank("sm")

        w_sb = sb("w_sb", [KT, DPROJ])
        wo_sb = sb("wo_sb", [XT, DIM])
        lnw_sb, lnb_sb = sb("lnw_sb", [KT]), sb("lnb_sb", [KT])
        lnb_bc = sb("lnb_bc", [KT, P])
        cw_sb, cb_sb = sb("cw_sb", [UT, TAPS]), sb("cb_sb", [UT])
        cbc_sb = sb("cbc_sb", [1])
        rms_sb = sb("rms_sb", [XT])
        alog_sb, a_sb, dsk_sb, dtb_sb = (sb(n, [HEADS]) for n in ("alog_sb", "a_sb", "dsk_sb", "dtb_sb"))
        ubias, zbias, dtbias = sb("ubias", [UT]), sb("zbias", [DINNER]), sb("dtbias", [HEADS])
        mean_w, ones, ident, tri, after = (sb(n, [P]) for n in ("mean_w", "ones", "ident", "tri", "after"))
        zeros = sb("zeros", [512])

        xb, xr = sb("xb", [2, KT, TOK]), sb("xr", [2, KT, TOK])
        xc, sq, rstd = sb("xc", [KT, TOK]), sb("sq", [KT, TOK]), sb("rstd", [2, TOK])
        xn = sb("xn", [4, KT, TOK])
        u = sb("u", [2, UT, ROWS + 2, PAD])
        acc = sb("acc", [UT, ROWS, IMG])
        pr = sb("pr", [2, len(AT), ROWS, IMG])
        xs = sb("xs", [2, XT, TOK])
        bt, ct = sb("bt", [2, TOK]), sb("ct", [2, TOK])
        z = sb("z", [2, CH, DINNER])
        dtv, dta, dt, da = (sb(n, [k, CH, HEADS]) for n, k in (("dtv", 4), ("dta", 4), ("dt", 4), ("da", 4)))
        dec = sb("dec", [4, 3, CH, HEADS])
        rr = sb("rr", [2, HEADS, P])
        em = sb("em", [2, HEADS, P])
        gm = sb("gm", [2, P])
        btok = sb("btok", [2, DSTATE])
        xdt, xd, dx = sb("xdt", [2, DINNER]), sb("xd", [2, DINNER]), sb("dx", [2, DINNER])
        yb = sb("yb", [2, DINNER])
        junk = sb("junk", [2, DINNER])
        rms = sb("rms", [2, 3])
        ynt = sb("ynt", [XT, TOK])
        st, sd = sb("st", [2, DINNER]), sb("sd", [DINNER])

        block = ctx.enter_context(nc.Block())

        def count(name, n, k=None):
            per = PER[name]
            k = per - 1 if k is None else k
            if n.known is not None:
                return n.known * per + k + 1 if n.known >= 0 else 0
            assert n.j >= 0, (name, n.j)
            return n.i * (GPB * per) + (n.j * per + k + 1)

        def chunk(n, c):
            return (n + c // CH, c % CH)

        def landed(n):
            if n.known is not None and n.known < 0:
                return 0
            return n.i * (GPB // 2 * 16) + 16 * (n.j // 2 + 1)

        def heads(ap, w=HD):
            return ap.rearrange("p (h d) -> p h d", h=HEADS)

        def per_head(ap, w=HD, rows=P):
            return ap.unsqueeze(2).to_broadcast([rows, HEADS, w])

        U, O, Z = (lambda m: ("u", 0, m, "u_ready")), (lambda m: ("o", -3, m, "out_ready")), (
            lambda c: ("z", -1, c, "z_biased"))
        MEAN, VAR = ("mean", 1, 0, "centered"), ("var", 1, 0, "lnvar")
        FILL = [([MEAN, U(0)], [U(1)]), ([U(2), U(3)], [VAR]), ([U(4), Z(0)], [O(0)]), ([O(1), Z(1)], [Z(2), Z(3)])]
        BIG = [use for pair in FILL for half in pair for use in half]
        NBIG = len(BIG)
        where = {(b[0], b[2]): q for q, b in enumerate(BIG)}

        def big_bank(t, what, part=0):
            return (t.j * NBIG + where[what, part]) % 2

        def big_free(eng, t, what, part=0):
            q = where[what, part] - 2
            s = t + (q // NBIG)
            kind, d, k, free = BIG[q % NBIG]
            if (s + d).exists:
                eng.wait_ge(sem[free], count(free, s + d, k))
            else:
                while (q // NBIG + t.known) >= -1:
                    q -= 2
                    s = t + (q // NBIG)
                    kind, d, k, free = BIG[q % NBIG]
                    if (s + d).exists:
                        eng.wait_ge(sem[free], count(free, s + d, k))
                        return

        @block.sync
        def _(sp):
            for dst, src in ((w_sb, w_in), (wo_sb, w_out), (lnw_sb, ln_w), (lnb_sb, ln_b), (cw_sb, conv_w),
                             (cb_sb, conv_b), (rms_sb, rms_w), (alog_sb, a_log), (dsk_sb, d_skip),
                             (dtb_sb, dt_bias)):
                sp.dma_start(dst[:], src).then_inc(w_loaded, 16)
            sp.dma_start(cbc_sb[0:DSTATE, :], conv_bc).then_inc(w_loaded, 16)

            def image(dram, n):
                g = n.j % GPB
                return dram[n.i + n.j // GPB, :, :, g * TOK:(g + 1) * TOK]

            def load(n):
                if n.exists:
                    sp.wait_ge(sem["centered"], count("centered", n - 2))
                    sp.dma_start(xb[:, n.j % 2], image(x, n)).then_inc(dma["x_loaded"][n.j % 2], 16)

            def step(t):
                if t.known == -1:
                    load(t + 1)
                load(t + 2)
                n = t - 2
                if n.exists:
                    sp.wait_ge(dma["out_stored"][(n - 2).j % 2], landed(n - 2))
                    sp.dma_start(xr[:, n.j % 2], image(x, n)).then_inc(dma["xr_loaded"][n.j % 2], 16)
                n = t - 3
                if n.exists:
                    sp.wait_ge(sem["out_ready"], count("out_ready", n))
                    sp.dma_start(image(out, n), xr[:, n.j % 2]).then_inc(dma["out_stored"][n.j % 2], 16)

            steps(sp, step)
            for stored in dma["out_stored"]:
                sp.wait_ge(stored, GROUPS // 2 * 16)

        @block.tensor
        def _(pe):
            pe.wait_ge(const_ready, 10)
            pe.wait_ge(w_loaded, 16 * 11)
            for m in range(UT):
                for k in range(KT):
                    last = pe.matmul(sm[:, 0, m:m + 1], w_sb[:, k, DINNER + m * P:DINNER + (m + 1) * P],
                                     lnb_sb[:, k:k + 1], start=k == 0, stop=k == KT - 1)
            last.then_inc(bias_done, 1)
            pe.wait_ge(w_scaled, 1)
            for lo, w, dst in ((0, DINNER, ydps[:, 0, :]), (DPROJ - HEADS, HEADS, yops[:, 0, 0:HEADS])):
                for k in range(KT):
                    last = pe.matmul(dst, lnb_bc[:, k, :], w_sb[:, k, lo:lo + w], start=k == 0, stop=k == KT - 1)
            last.then_inc(bias_done, 1)
            pe.wait_ge(w_scaled, 4)

            def mean(t):
                n = t + 1
                if n.exists:
                    pe.wait_ge(dma["x_loaded"][n.j % 2], landed(n))
                    big_free(pe, t, "mean")
                    for k in range(KT):
                        last = pe.matmul(big[:, big_bank(t, "mean"), :], mean_w[:], xb[:, n.j % 2, k, :],
                                         start=k == 0, stop=k == KT - 1)
                    last.then_inc(sem["mean_done"], 1)

            def var(t):
                n = t + 1
                if n.exists:
                    pe.wait_ge(sem["squared"], count("squared", n))
                    big_free(pe, t, "var")
                    for k in range(KT):
                        last = pe.matmul(big[:, big_bank(t, "var"), :], mean_w[:], sq[:, k, :],
                                         start=k == 0, stop=k == KT - 1)
                    last.then_inc(sem["var_done"], 1)

            def project_u(t, m):
                if t.exists:
                    if m == 0:
                        pe.wait_ge(sem["xn_ready"], count("xn_ready", t))
                    big_free(pe, t, "u", m)
                    for k in range(KT):
                        last = pe.matmul(big[:, big_bank(t, "u", m), :],
                                         w_sb[:, k, DINNER + m * P:DINNER + (m + 1) * P], xn[:, t.j % 4, k, :],
                                         start=k == 0, stop=k == KT - 1)
                    last.then_inc(sem["u_done"], 1)

            def project_z(t, c):
                n = t - 1
                if n.exists:
                    big_free(pe, t, "z", c)
                    for k in range(KT):
                        last = pe.matmul(big[:, big_bank(t, "z", c), :], xn[:, n.j % 4, k, c * P:(c + 1) * P],
                                         w_sb[:, k, 0:DINNER], start=k == 0, stop=k == KT - 1)
                    last.then_inc(sem["z_done"], 1)

            def project_dt(t):
                if t.exists:
                    pe.wait_ge(sem["btok_ready"], count("btok_ready", t - 2, CH - 2))
                    if t.known is not None and 0 < t.known < 2:
                        pe.wait_ge(sem["dec_ready"], count("dec_ready", t - 1))
                    for c in range(CH):
                        for k in range(KT):
                            last = pe.matmul(sm[:, 0, c * HEADS:(c + 1) * HEADS],
                                             xn[:, t.j % 4, k, c * P:(c + 1) * P], w_sb[:, k, DPROJ - HEADS:],
                                             start=k == 0, stop=k == KT - 1)
                    last.then_inc(sem["dt_done"], 1)

            def decays(t):
                n = t - 1
                if n.exists:
                    pe.wait_ge(sem["da_ready"], count("da_ready", n))
                    pe.wait_ge(sem["dt_biased"], count("dt_biased", n))
                    pe.wait_ge(sem["btok_ready"], count("btok_ready", *chunk(t - 2, -1)))
                    for k, w in enumerate((tri, after, ones)):
                        last = pe.matmul(sm[:, 0, 32 * k:32 * k + 32], w[:],
                                         da[:, n.j % 4].rearrange("p c h -> p (c h)"), start=True, stop=True)
                    last.then_inc(sem["decay_done"], 1)

            def project_out(t, m):
                n = t - 3
                if n.exists:
                    if m == 0:
                        pe.wait_ge(sem["ynt_ready"], count("ynt_ready", n))
                    big_free(pe, t, "o", m)
                    for k in range(XT):
                        last = pe.matmul(big[:, big_bank(t, "o", m), :], wo_sb[:, k, m * P:(m + 1) * P],
                                         ynt[:, k, :], start=k == 0, stop=k == XT - 1)
                    last.then_inc(sem["o_done"], 1)

            def first(t, c):
                n, k = chunk(t - 2, c)
                if not n.exists:
                    return
                tok = slice(k * P, (k + 1) * P)
                if k == 0:
                    pe.wait_ge(sem["conv_ready"], count("conv_ready", n))
                pe.wait_ge(sem["e_ready"], count("e_ready", *chunk(n, k - 1)))
                pe.wait_ge(sem["r_ready"], count("r_ready", n, k))
                for j in range(2):
                    last = pe.matmul(dps[:, j, :], after[:],
                                     rr[:, k % 2, 4 * j:4 * j + 4, :].rearrange("p h q -> p (h q)"),
                                     start=True, stop=True)
                last.then_inc(sem["d_done"], 1)
                if c == -1:
                    pe.wait_ge(sem["dt_biased"], count("dt_biased", t - 1 if (t - 1).exists else n))
                if c == 0:
                    pe.wait_ge(sem["dec_ready"], count("dec_ready", t - 1 if (t - 1).exists else n))
                pe.wait_ge(sem["btok_ready"], count("btok_ready", *chunk(n, k - 1)))
                pe.matmul(sm[:, 0, 0:P], bt[0:DSTATE, n.j % 2, tok], ct[0:DSTATE, n.j % 2, tok],
                          start=True, stop=True)
                pe.transpose(sm[:, 0, P:P + DSTATE], bt[0:DSTATE, n.j % 2, tok],
                             ident[0:DSTATE, 0:DSTATE]).then_inc(sem["gb_done"], 1)
                pe.wait_ge(sem["ynt_ready"], count("ynt_ready", *chunk(n, k - 2)))
                pe.wait_ge(sem["dx_ready"], count("dx_ready", *chunk(n, k - 1)))
                for j in range(XT):
                    last = pe.transpose(tps[:, 0, j * P:(j + 1) * P], xs[:, n.j % 2, j, tok], ident[:])
                last.then_inc(sem["xt_done"], 1)

            def off(t, c):
                n, k = chunk(t - 2, c - 1)
                if not n.exists:
                    return
                start = n.j % GPB == 0 and k == 0
                pe.wait_ge(sem["s_ready"], count("s_ready", *chunk(n, k - 1)))
                s = zeros if start else st[:, (k - 1) % 2]
                pe.matmul(yops[:, 0, :], ct[0:DSTATE, n.j % 2, k * P:(k + 1) * P], s[0:DSTATE, :],
                          start=True, stop=True).then_inc(sem["yoff_done"], 1)

            def diag(t, c):
                n, k = chunk(t - 2, c - 1)
                if not n.exists:
                    return
                pe.wait_ge(sem["m_ready"], count("m_ready", n, k))
                pe.wait_ge(sem["y_summed"], count("y_summed", *chunk(n, k - 1)))
                for h in range(HEADS):
                    last = pe.matmul(ydps[:, 0, h * HD:(h + 1) * HD], em[:, k % 2, h, :],
                                     xdt[:, k % 2, h * HD:(h + 1) * HD], start=True, stop=True)
                last.then_inc(sem["ydiag_done"], 1)

            def state(t, c):
                n, k = chunk(t - 2, c - 1)
                if not n.exists:
                    return
                pe.wait_ge(sem["xd_ready"], count("xd_ready", n, k))
                pe.wait_ge(sem["yoff_scaled"], count("yoff_scaled", n, k))
                pe.matmul(yops[0:DSTATE, 0, :], btok[:, k % 2, :], xd[:, k % 2, :],
                          start=True, stop=True).then_inc(sem["state_done"], 1)

            def turn(t, c):
                n, k = chunk(t - 2, c - 2)
                if not n.exists:
                    return
                pe.wait_ge(sem["yn_ready"], count("yn_ready", n, k))
                m, q = chunk(t - 2, c - 1)
                if m.exists:
                    pe.wait_ge(sem["dx_ready"], count("dx_ready", m, q))
                else:
                    pe.wait_ge(sem["ynt_ready"], count("ynt_ready", *chunk(n, k - 1)))
                for j in range(XT):
                    last = pe.transpose(tps[:, 0, j * P:(j + 1) * P], yb[:, k % 2, j * P:(j + 1) * P], ident[:])
                last.then_inc(sem["yt_done"], 1)

            def fill(t, uses):
                for what, _, part, _ in uses:
                    if what in ("mean", "var"):
                        {"mean": mean, "var": var}[what](t)
                    else:
                        {"u": project_u, "o": project_out, "z": project_z}[what](t, part)

            def step(t):
                for c in range(CH):
                    fill(t, FILL[c][0])
                    if c == 1:
                        decays(t)
                    off(t, c - 1)
                    diag(t, c - 1)
                    turn(t, c - 1)
                    first(t, c - 1)
                    fill(t, FILL[c][1])
                    if c == CH - 1:
                        project_dt(t)
                    state(t, c - 1)

            steps(pe, step)

        @block.scalar
        def _(act):
            act.wait_ge(w_loaded, 16 * 11)
            act.activation(a_sb[:], alog_sb[:], ACT.Exp).then_inc(a_exp, 1)
            act.wait_ge(const_ready, 10)

            def square(t):
                n = t + 1
                if n.exists:
                    act.wait_ge(sem["centered"], count("centered", n))
                    act.wait_ge(sem["var_done"], count("var_done", n - 1))
                    act.activation(sq[:], xc[:], ACT.Square).then_inc(sem["squared"], 1)

            def rstd_of(t):
                n = t + 1
                if n.exists:
                    act.wait_ge(sem["var_done"], count("var_done", n))
                    act.activation(rstd[:, 0, :], big[:, big_bank(t, "var"), :], ACT.Ln, bias=EPS).then_inc(
                        sem["lnvar"], 1)
                    act.wait_ge(sem["lnvar"], count("lnvar", n))
                    act.wait_ge(sem["xn_ready"], count("xn_ready", n - 1))
                    act.activation(rstd[:, 1, :], rstd[:, 0, :], ACT.Exp, scale=-0.5).then_inc(sem["rstd_ready"], 1)

            def top(t):
                n = t
                if n.exists:
                    act.wait_ge(sem["conv_step"], count("conv_step", n - 2))
                    act.wait_ge(sem["u_ready"], count("u_ready", n - 1))
                    dst = u[:, n.j % 2, :, 0, 1:IMG + 1]
                    if n.j % GPB == 0:
                        src = zeros[:, 0:UT * IMG].rearrange("p (m w) -> p m w", m=UT)
                    else:
                        src = u[:, (n.j - 1) % 2, :, ROWS, 1:IMG + 1]
                    act.activation(dst, src, ACT.Copy).then_inc(sem["top_halo"], 1)

            def u_rows(t, m):
                n = t
                if n.exists:
                    act.wait_ge(sem["u_done"], count("u_done", n, m))
                if (n - 1).exists:
                    dst = u[:, (n.j - 1) % 2, m, ROWS + 1, 1:IMG + 1]
                    if n.j % GPB == 0:
                        i = act.activation(dst, zeros[:, 0:IMG], ACT.Copy)
                    else:
                        i = act.activation(dst, big[:, big_bank(t, "u", m), 0:IMG], ACT.Identity,
                                           bias=ubias[:, m:m + 1])
                    i.then_inc(sem["bottom_halo"], 1)
                elif n.known == 0:
                    act.activation(junk[:, 0, 0:IMG], zeros[:, 0:IMG], ACT.Copy).then_inc(sem["bottom_halo"], 1)
                    if m < UT - 1:
                        act.wait_ge(sem["bottom_halo"], count("bottom_halo", n, m))
                if n.exists:
                    act.activation(u[:, n.j % 2, m, 1:ROWS + 1, 1:IMG + 1],
                                   big[:, big_bank(t, "u", m), :].rearrange("p (r w) -> p r w", r=ROWS),
                                   ACT.Identity, bias=ubias[:, m:m + 1]).then_inc(sem["u_ready"], 1)

            def softplus(t):
                n = t
                if n.exists:
                    act.wait_ge(sem["dt_biased"], count("dt_biased", n))
                    v, a = dtv[:, n.j % 4], dta[:, n.j % 4]
                    act.activation(a, v, ACT.Abs).then_inc(sem["dt_abs"], 1)
                    act.wait_ge(sem["dt_abs"], count("dt_abs", n))
                    act.activation(a, a, ACT.Exp, scale=-1.0).then_inc(sem["dt_exp"], 1)
                    act.wait_ge(sem["dt_exp"], count("dt_exp", n))
                    act.activation(a, a, ACT.Ln, bias=1.0).then_inc(sem["dt_log"], 1)

            def decays(t):
                n = t - 1
                if n.exists:
                    act.wait_ge(sem["decay_done"], count("decay_done", n))
                    act.activation(dec[:, n.j % 4].rearrange("p k c h -> p (k c h)"), sm[:, 0, 0:96],
                                   ACT.Exp).then_inc(sem["dec_ready"], 1)

            def exps(t, c):
                n, k = chunk(t - 2, c)
                if n.exists:
                    act.wait_ge(sem["d_done"], count("d_done", n, k))
                    act.wait_ge(sem["ydiag_done"], count("ydiag_done", *chunk(n, k - 2)))
                    act.activation(em[:, k % 2].rearrange("p h q -> p (h q)"),
                                   dps[:].rearrange("p k q -> p (k q)"), ACT.Exp).then_inc(sem["e_ready"], 1)

            def rms_of(t, c):
                n, k = chunk(t - 2, c - 1)
                if n.exists:
                    act.wait_ge(sem["y_gated"], count("y_gated", n, k))
                    act.wait_ge(sem["yn_ready"], count("yn_ready", *chunk(n, k - 2)))
                    act.activation(junk[:, k % 2, :], yb[:, k % 2, :], ACT.Square,
                                   accum_out=rms[:, k % 2, 0:1]).then_inc(sem["ss_ready"], 1)
                    act.wait_ge(sem["ss_ready"], count("ss_ready", n, k))
                    act.activation(rms[:, k % 2, 1:2], rms[:, k % 2, 0:1], ACT.Ln, bias=EPS,
                                   scale=1.0 / DINNER).then_inc(sem["rms_log"], 1)
                    act.wait_ge(sem["rms_log"], count("rms_log", n, k))
                    act.activation(rms[:, k % 2, 2:3], rms[:, k % 2, 1:2], ACT.Exp, scale=-0.5).then_inc(
                        sem["rms_ready"], 1)

            def turned(t, c):
                n, k = chunk(t - 2, c - 2)
                if n.exists:
                    act.wait_ge(sem["yt_done"], count("yt_done", n, k))
                    if k == 0:
                        act.wait_ge(sem["o_done"], count("o_done", n - 1))
                    act.activation(ynt[:, :, k * P:(k + 1) * P],
                                   tps[:, 0, :].rearrange("p (j q) -> p j q", j=XT),
                                   ACT.Copy).then_inc(sem["ynt_ready"], 1)

            def silu_conv(t):
                n = t - 2
                if not n.exists:
                    return
                act.wait_ge(sem["yoff_done"], count("yoff_done", n - 2))
                for m in range(XT):
                    act.wait_ge(sem["conv_step"], count("conv_step", n, (TAPS - 1) * len(VT) + m))
                    act.activation(xs[:, n.j % 2, m, :], acc[:, m].rearrange("p r w -> p (r w)"), ACT.Silu,
                                   bias=cb_sb[:, m:m + 1]).then_inc(sem["conv_ready"], 1)
                act.wait_ge(sem["tap_added"], count("tap_added", n))
                for dst, rows, bias in ((bt, slice(0, DSTATE), cb_sb[0:DSTATE, XT:UT]),
                                        (ct, slice(DSTATE, P), cb_sb[DSTATE:P, XT:UT])):
                    act.activation(dst[0:DSTATE, n.j % 2, :], acc[rows, XT].rearrange("p r w -> p (r w)"),
                                   ACT.Silu, bias=cbc_sb[0:DSTATE, :] if dst is ct else bias).then_inc(
                                       sem["conv_ready"], 1)

            def silu_z(t, c):
                n = t - 2
                if n.exists:
                    act.wait_ge(sem["z_biased"], count("z_biased", n, c))
                    act.activation(z[:, n.j % 2, c, :], z[:, n.j % 2, c, :], ACT.Silu).then_inc(sem["z_ready"], 1)

            def taps(t, lo, hi):
                n = t - 1
                if not n.exists:
                    return
                for q in range(lo, hi):
                    tap, a = divmod(q, len(AT))
                    m = AT[a]
                    dy, dx_ = divmod(tap, 3)
                    if q == 0:
                        act.wait_ge(sem["top_halo"], count("top_halo", n))
                        act.wait_ge(sem["u_ready"], count("u_ready", n))
                        act.wait_ge(sem["conv_ready"], count("conv_ready", n - 1))
                    if dy == 2 and dx_ == 0:
                        act.wait_ge(sem["bottom_halo"], count("bottom_halo", n + 1, m))
                    if tap > 2:
                        act.wait_ge(sem["tap_added"], count("tap_added", n, q - 3 * len(AT)))
                    elif tap:
                        act.wait_ge(sem["tap_added"], count("tap_added", n - 1))
                    dst = pr[:, tap % 2, a] if tap else acc[:, m]
                    act.activation(dst, u[:, n.j % 2, m, dy:dy + ROWS, dx_:dx_ + IMG], ACT.Copy,
                                   scale=cw_sb[:, m, tap:tap + 1]).then_inc(sem["tap_made"], 1)

            def step(t):
                softplus(t - 1)
                silu_conv(t)
                for c in range(CH):
                    if c == 1:
                        decays(t)
                    for what, _, part, _ in FILL[c][0]:
                        if what == "u":
                            if part == 0:
                                top(t)
                            u_rows(t, part)
                    if c == 0:
                        square(t)
                    turned(t, c - 1)
                    if c == 0:
                        for k in range(CH):
                            silu_z(t, k)
                        act.preload_act_table_set("natural_log_exp_and_others")
                    taps(t, *((0, 2), (3, 4), (5, 6), (7, 8))[c])
                    exps(t, c - 1)
                    for what, _, part, _ in FILL[c][1]:
                        if what == "u":
                            u_rows(t, part)
                        if what == "var":
                            rstd_of(t)
                    rms_of(t, c - 1)
                    taps(t, *((2, 3), (4, 5), (6, 7), (8, 9))[c])

            steps(act, step)

        @block.vector
        def _(dve):
            dve.wait_ge(w_loaded, 16 * 11)
            for k in range(KT):
                i = dve.tensor_copy(lnb_bc[:, k, :], lnb_sb[:, k:k + 1].to_broadcast([P, P]))
            i.then_inc(w_scaled, 1)
            dve.wait_ge(bias_done, 2)
            for k in range(KT):
                i = dve.tensor_scalar(w_sb[:, k, :], w_sb[:, k, :], lnw_sb[:, k:k + 1], None, ALU.mult)
            i.then_inc(w_scaled, 1)
            for k in range(XT):
                i = dve.tensor_scalar(wo_sb[:, k, :], wo_sb[:, k, :], rms_sb[:, k:k + 1], None, ALU.mult)
            i.then_inc(w_scaled, 1)
            dve.tensor_copy(ubias[:], sm[:, 0, 0:UT]).then_inc(bias_ready, 1)
            dve.tensor_copy(zbias[:], ydps[:, 0, :]).then_inc(bias_ready, 1)
            dve.tensor_tensor(dtbias[:], dtb_sb[:], yops[:, 0, 0:HEADS], ALU.add).then_inc(bias_ready, 1)
            dve.wait_ge(a_exp, 1)
            dve.tensor_scalar(a_sb[:], a_sb[:], -1.0, None, ALU.mult).then_inc(bias_ready, 1)
            dve.wait_ge(bias_ready, 4)
            dve.nop().then_inc(w_scaled, 1)
            dve.wait_ge(const_ready, 10)

            def center(t):
                n = t + 1
                if n.exists:
                    dve.wait_ge(sem["mean_done"], count("mean_done", n))
                    dve.wait_ge(sem["xn_ready"], count("xn_ready", n - 1))
                    dve.tensor_tensor(xc[:], xb[:, n.j % 2],
                                      big[:, big_bank(t, "mean"), :].unsqueeze(1).to_broadcast([P, KT, TOK]),
                                      ALU.subtract).then_inc(sem["centered"], 1)

            def z_bias(t, c):
                n = t - 1
                if n.exists:
                    dve.wait_ge(sem["z_done"], count("z_done", n, c))
                    dve.wait_ge(sem["y_gated"], count("y_gated", n - 2, c))
                    dve.tensor_tensor(z[:, n.j % 2, c, :], big[:, big_bank(t, "z", c), :], zbias[:],
                                      ALU.add).then_inc(sem["z_biased"], 1)

            def dt_bias_add(t):
                n = t
                if n.exists:
                    dve.wait_ge(sem["dt_done"], count("dt_done", n))
                    dve.tensor_tensor(dtv[:, n.j % 4], sm[:, 0, 0:32].rearrange("p (c h) -> p c h", c=CH),
                                      dtbias[:].unsqueeze(1).to_broadcast([P, CH, HEADS]),
                                      ALU.add).then_inc(sem["dt_biased"], 1)

            def dt_end(t):
                n = t
                if n.exists:
                    dve.wait_ge(sem["dt_log"], count("dt_log", n))
                    dve.scalar_tensor_tensor(dt[:, n.j % 4], dtv[:, n.j % 4], 0.0, dta[:, n.j % 4],
                                             ALU.max, ALU.add).then_inc(sem["dt_ready"], 1)
                    dve.wait_ge(sem["dt_ready"], count("dt_ready", n))
                    dve.tensor_tensor(da[:, n.j % 4], dt[:, n.j % 4],
                                      a_sb[:].unsqueeze(1).to_broadcast([P, CH, HEADS]),
                                      ALU.mult).then_inc(sem["da_ready"], 1)

            def x_tokens(t, c):
                n, k = chunk(t - 2, c)
                if n.exists:
                    dve.wait_ge(sem["xt_done"], count("xt_done", n, k))
                    dve.wait_ge(sem["xd_ready"], count("xd_ready", *chunk(n, k - 2)))
                    dve.wait_ge(sem["ydiag_done"], count("ydiag_done", *chunk(n, k - 2)))
                    dve.tensor_tensor(heads(xdt[:, k % 2, :]), heads(tps[:, 0, :]),
                                      per_head(dt[:, n.j % 4, k, :]), ALU.mult).then_inc(sem["xdt_ready"], 1)
                    dve.wait_ge(sem["yd_added"], count("yd_added", *chunk(n, k - 2)))
                    dve.tensor_tensor(heads(dx[:, k % 2, :]), heads(tps[:, 0, :]), per_head(dsk_sb[:]),
                                      ALU.mult).then_inc(sem["dx_ready"], 1)

            def small(t, c):
                n, k = chunk(t - 2, c)
                if n.exists:
                    dve.wait_ge(sem["gb_done"], count("gb_done", n, k))
                    dve.wait_ge(sem["m_ready"], count("m_ready", *chunk(n, k - 2)))
                    dve.tensor_tensor(gm[:, k % 2, :], sm[:, 0, 0:P], tri[:], ALU.mult).then_inc(sem["gm_ready"], 1)
                    dve.wait_ge(sem["state_done"], count("state_done", *chunk(n, k - 2)))
                    dve.tensor_copy(btok[:, k % 2, :], sm[:, 0, P:P + DSTATE]).then_inc(sem["btok_ready"], 1)

            def masked(t, c):
                n, k = chunk(t - 2, c)
                if n.exists:
                    dve.wait_ge(sem["e_ready"], count("e_ready", n, k))
                    dve.wait_ge(sem["gm_ready"], count("gm_ready", n, k))
                    dve.tensor_tensor(em[:, k % 2], em[:, k % 2],
                                      gm[:, k % 2, :].unsqueeze(1).to_broadcast([P, HEADS, P]),
                                      ALU.mult).then_inc(sem["m_ready"], 1)

            def off_scale(t, c):
                n, k = chunk(t - 2, c - 1)
                if n.exists:
                    dve.wait_ge(sem["yoff_done"], count("yoff_done", n, k))
                    dve.wait_ge(sem["yt_done"], count("yt_done", *chunk(n, k - 2)))
                    dve.tensor_tensor(heads(yb[:, k % 2, :]), heads(yops[:, 0, :]),
                                      per_head(dec[:, n.j % 4, 0, k, :]), ALU.mult).then_inc(sem["yoff_scaled"], 1)

            def sum_y(t, c):
                n, k = chunk(t - 2, c - 1)
                if n.exists:
                    dve.wait_ge(sem["ydiag_done"], count("ydiag_done", n, k))
                    dve.wait_ge(sem["yd_added"], count("yd_added", n, k))
                    dve.tensor_tensor(yb[:, k % 2, :], yb[:, k % 2, :], ydps[:, 0, :],
                                      ALU.add).then_inc(sem["y_summed"], 1)

            def new_state(t, c):
                n, k = chunk(t - 2, c - 1)
                if n.exists:
                    dve.wait_ge(sem["state_done"], count("state_done", n, k))
                    dve.wait_ge(sem["s_decayed"], count("s_decayed", n, k))
                    dve.tensor_tensor(st[0:DSTATE, k % 2, :], sd[0:DSTATE, :], yops[0:DSTATE, 0, :],
                                      ALU.add).then_inc(sem["s_ready"], 1)

            def normalise(t, c):
                n, k = chunk(t - 2, c - 2)
                if n.exists:
                    dve.wait_ge(sem["rms_ready"], count("rms_ready", n, k))
                    dve.tensor_scalar(yb[:, k % 2, :], yb[:, k % 2, :], rms[:, k % 2, 2:3], None,
                                      ALU.mult).then_inc(sem["yn_ready"], 1)

            def finish(t, m):
                n = t - 3
                if n.exists:
                    dve.wait_ge(sem["o_done"], count("o_done", n, m))
                    if m == 0:
                        dve.wait_ge(dma["xr_loaded"][n.j % 2], landed(n))
                    dve.tensor_tensor(xr[:, n.j % 2, m, :], xr[:, n.j % 2, m, :],
                                      big[:, big_bank(t, "o", m), :], ALU.add).then_inc(sem["out_ready"], 1)

            def convolve(t, lo, hi):
                n = t - 1
                if not n.exists:
                    return
                for q in range(lo, hi):
                    tap, m = divmod(q, len(VT))
                    m = VT[m]
                    dy, dx_ = divmod(tap, 3)
                    if q == 0:
                        dve.wait_ge(sem["top_halo"], count("top_halo", n))
                        dve.wait_ge(sem["u_ready"], count("u_ready", n))
                    if dy == 2 and dx_ == 0:
                        dve.wait_ge(sem["bottom_halo"], count("bottom_halo", n + 1, m))
                    src = u[:, n.j % 2, m, dy:dy + ROWS, dx_:dx_ + IMG]
                    w = cw_sb[:, m, tap:tap + 1]
                    if tap:
                        dve.wait_ge(sem["conv_step"], count("conv_step", n, q - len(VT)))
                    else:
                        dve.wait_ge(sem["conv_ready"], count("conv_ready", n - 1, m))
                    other = acc[:, m] if tap else zeros[:].rearrange("p (r w) -> p r w", r=ROWS)
                    dve.scalar_tensor_tensor(acc[:, m], src, w, other, ALU.mult, ALU.add).then_inc(
                        sem["conv_step"], 1)

            def step(t):
                for c in range(CH):
                    normalise(t, c - 1)
                    if c == 0:
                        center(t)
                    if c == 2:
                        z_bias(t, 0)
                    if c == 3:
                        finish(t, 1)
                    off_scale(t, c - 1)
                    if c == 0:
                        dt_end(t - 1)
                    if c == 3:
                        z_bias(t, 1)
                    convolve(t, 9 * c, 9 * c + 3)
                    sum_y(t, c - 1)
                    small(t, c - 1)
                    x_tokens(t, c - 1)
                    if c == 2:
                        finish(t, 0)
                    if c == 3:
                        z_bias(t, 2)
                    convolve(t, 9 * c + 3, 9 * c + 6)
                    if c == 3:
                        z_bias(t, 3)
                        dt_bias_add(t)
                    new_state(t, c - 1)
                    masked(t, c - 1)
                    convolve(t, 9 * c + 6, 9 * c + 9)

            steps(dve, step)

        @block.gpsimd
        def _(pool):
            pool.memset(mean_w[:], 1.0 / DIM).then_inc(const_ready, 1)
            pool.memset(ones[:], 1.0).then_inc(const_ready, 1)
            pool.memset(zeros[:], 0.0).then_inc(const_ready, 1)
            pool.memset(u[:], 0.0).then_inc(const_ready, 1)
            for c in (ident, tri, after):
                last = pool.memset(c[:], 1.0)
            last.then_inc(const_ready, 1)
            pool.wait_ge(const_ready, 5)
            pool.affine_select(out=ident[:], in_=ident[:], compare_op=ALU.is_equal, fill=0.0, base=0,
                               pattern=[[-1, P]], channel_multiplier=1).then_inc(const_ready, 1)
            pool.affine_select(out=tri[:], in_=tri[:], compare_op=ALU.is_ge, fill=0.0, base=0,
                               pattern=[[1, P]], channel_multiplier=-1).then_inc(const_ready, 1)
            pool.affine_select(out=after[:], in_=after[:], compare_op=ALU.is_gt, fill=0.0, base=0,
                               pattern=[[-1, P]], channel_multiplier=1).then_inc(const_ready, 1)
            pool.memset(yb[:], 0.0).then_inc(const_ready, 1)
            pool.wait_ge(const_ready, 9)
            pool.memset(junk[:], 0.0).then_inc(const_ready, 1)
            pool.wait_ge(const_ready, 10)
            pool.wait_ge(w_loaded, 16 * 11)

            def product(out_, a, b, name, op=ALU.mult):
                pool.tensor_tensor(out_, a, b, op).then_inc(sem[name], 1)

            def norm(t):
                n = t + 1
                if n.exists:
                    pool.wait_ge(sem["rstd_ready"], count("rstd_ready", n))
                    pool.wait_ge(sem["z_done"], count("z_done", n - 4))
                    product(xn[:, n.j % 4], xc[:], rstd[:, 1, :].unsqueeze(1).to_broadcast([P, KT, TOK]),
                            "xn_ready")

            def ramps(t, c):
                n, k = chunk(t - 2, c + 1)
                if n.exists:
                    if k == 0:
                        pool.wait_ge(sem["da_ready"], count("da_ready", n))
                    pool.wait_ge(sem["d_done"], count("d_done", *chunk(n, k - 2)))
                    product(rr[:, k % 2], tri[:].unsqueeze(1).to_broadcast([P, HEADS, P]),
                            per_head(da[:, n.j % 4, k, :], P), "r_ready")

            def skip(t, c):
                n, k = chunk(t - 2, c - 1)
                if n.exists:
                    pool.wait_ge(sem["yoff_scaled"], count("yoff_scaled", n, k))
                    product(yb[:, k % 2, :], yb[:, k % 2, :], dx[:, k % 2, :], "yd_added", ALU.add)

            def decayed_x(t, c):
                n, k = chunk(t - 2, c)
                if n.exists:
                    pool.wait_ge(sem["xdt_ready"], count("xdt_ready", n, k))
                    pool.wait_ge(sem["state_done"], count("state_done", *chunk(n, k - 2)))
                    product(heads(xd[:, k % 2, :]), heads(xdt[:, k % 2, :]), per_head(dec[:, n.j % 4, 1, k, :]),
                            "xd_ready")

            def decayed_state(t, c):
                n, k = chunk(t - 2, c - 1)
                if n.exists:
                    pool.wait_ge(sem["s_ready"], count("s_ready", *chunk(n, k - 1)))
                    start = n.j % GPB == 0 and k == 0
                    s = zeros[0:DSTATE, :] if start else st[0:DSTATE, (k - 1) % 2, :]
                    product(heads(sd[0:DSTATE, :]), heads(s), per_head(dec[0:DSTATE, n.j % 4, 2, k, :], rows=DSTATE),
                            "s_decayed")

            def gate(t, c):
                n, k = chunk(t - 2, c - 1)
                if n.exists:
                    pool.wait_ge(sem["y_summed"], count("y_summed", n, k))
                    pool.wait_ge(sem["z_ready"], count("z_ready", n, k))
                    product(yb[:, k % 2, :], yb[:, k % 2, :], z[:, n.j % 2, k, :], "y_gated")

            def add_taps(t, lo, hi):
                n = t - 1
                if n.exists:
                    for q in range(lo, hi):
                        tap, a = divmod(q, len(AT))
                        pool.wait_ge(sem["tap_made"], count("tap_made", n, q + len(AT)))
                        if tap:
                            pool.wait_ge(sem["tap_added"], count("tap_added", n, q - len(AT)))
                        product(acc[:, AT[a]], acc[:, AT[a]], pr[:, (tap + 1) % 2, a], "tap_added", ALU.add)

            def step(t):
                for c in range(CH):
                    decayed_state(t, c - 1)
                    skip(t, c - 1)
                    add_taps(t, 2 * c, 2 * c + 1)
                    gate(t, c - 1)
                    decayed_x(t, c - 1)
                    ramps(t, c - 1)
                    if c == 2:
                        norm(t)
                    add_taps(t, 2 * c + 1, 2 * c + 2)

            steps(pool, step)


def kernel(x, L0_conv_ln_w, L0_conv_ln_b, L0_conv_in_proj_w, L0_conv_conv_w, L0_conv_conv_b, L0_conv_A_log,
           L0_conv_D, L0_conv_dt_bias, L0_conv_rms_w, L0_conv_out_proj_w):
    import concourse.bacc as bacc
    from concourse.bass_utils import run_bass_kernel_spmd

    def rows(a, n):
        a = np.asarray(a)
        return np.ascontiguousarray(np.moveaxis(a.reshape(n, P, *a.shape[1:]), 0, 1))

    def everywhere(a):
        return np.ascontiguousarray(np.broadcast_to(np.asarray(a), (P, a.shape[0])))

    xv = np.ascontiguousarray(np.asarray(x).reshape(B, KT, P, IMG * IMG).transpose(0, 2, 1, 3))
    arrays = {
        "x": xv,
        "w_in": rows(np.asarray(L0_conv_in_proj_w).T, KT),
        "ln_w": rows(L0_conv_ln_w, KT), "ln_b": rows(L0_conv_ln_b, KT),
        "conv_w": rows(np.asarray(L0_conv_conv_w).reshape(UT * P, TAPS), UT), "conv_b": rows(L0_conv_conv_b, UT),
        "conv_bc": np.ascontiguousarray(np.asarray(L0_conv_conv_b)[-DSTATE:, None]),
        "a_log": everywhere(L0_conv_A_log), "d_skip": everywhere(L0_conv_D),
        "dt_bias": everywhere(L0_conv_dt_bias),
        "rms_w": rows(L0_conv_rms_w, XT), "w_out": rows(np.asarray(L0_conv_out_proj_w).T, XT),
    }
    nc = bacc.Bacc("TRN2", target_bir_lowering=False, num_devices=1)
    args = [nc.dram_tensor(f"in_{k}", a.shape, mybir.dt.from_np(a.dtype), kind="ExternalInput").ap()
            for k, a in arrays.items()]
    out = nc.dram_tensor("out", xv.shape, F32, kind="ExternalOutput").ap()
    build(nc, *args, out)
    r = run_bass_kernel_spmd(nc, [{f"in_{k}": a for k, a in arrays.items()}], core_ids=[0])
    got = r.results[0]["out"]
    return np.ascontiguousarray(got.transpose(0, 2, 1, 3)).reshape(B, DIM, IMG, IMG)
```

```python
import numpy as np

from concourse import mybir
from concourse.alu_op_type import AluOpType as ALU

F32 = mybir.dt.float32
BF16 = mybir.dt.bfloat16
F16 = mybir.dt.float16
ACT = mybir.ActivationFunctionType

P = 128
B, DIM, IMG = 8, 256, 64
DINNER, DSTATE, HEADS = 512, 64, 8
HD = DINNER // HEADS
KT = DIM // P
UT = (DINNER + 2 * DSTATE) // P
XT = DINNER // P
DPROJ = 2 * DINNER + 2 * DSTATE + HEADS
ROWS = 8
TOK = ROWS * IMG
CH = TOK // P
GPB = IMG // ROWS
GROUPS = B * GPB
PAD = IMG + 2
EPS = 1e-5
CONSTS = 25
TAPS = 9
VT = (0, 1, 2)
AT = (3, 4)
PIECES = 3
XSCALE, YSCALE = 64.0, 32.0
WMAX = 1024.0
TINY = 1e-30
SPLIT = ((0, 0), (0, 1), (1, 0))
NEVER = -2.0 ** 100
PER = dict(
    mean_done=1, var_done=1, u_done=UT, z_done=CH, dt_done=1, decay_done=1, xt_done=CH, gb_done=CH, d_done=CH,
    ydiag_done=CH, yoff_done=CH, state_done=CH, yt_done=CH, o_done=2,
    centered=1, xc_scaled=1, xn_hi=1, z_biased=CH, dt_biased=1, dt_ready=1, da_ready=1, xdt_ready=CH, dx_ready=CH,
    gb_ready=CH, yoff_scaled=CH, m_ready=CH, y_summed=CH, yn_ready=CH, s_ready=CH, out_ready=2,
    conv_step=TAPS * len(VT), tap_made=TAPS * len(AT), tap_added=(TAPS - 1) * len(AT),
    xn_ready=1, acs_done=1, acs_hi=1, acs_rest=1, acs_mid=1, acs_lo=1, yd_added=CH, xd_ready=CH, s_decayed=CH,
    y_gated=CH,
    squared=1, lnvar=1, rstd_ready=1, u_ready=UT, top_halo=1, bottom_halo=UT, dt_abs=1, dt_exp=1, dt_log=1,
    dec_ready=1, e_ready=CH, ss_ready=CH, rms_log=CH, rms_ready=CH, yt_hi=CH, ynt_ready=CH, z_ready=CH,
    conv_ready=UT + 1,
)


class At:

    def __init__(self, j, i):
        self.j, self.i = j, i

    def __add__(self, k):
        return At(self.j + k, self.i)

    def __sub__(self, k):
        return At(self.j - k, self.i)

    @property
    def known(self):
        return self.j + GPB * self.i if isinstance(self.i, int) else None

    @property
    def exists(self):
        return self.known is None or 0 <= self.known < GROUPS


J0 = 5
LOOPS = (GROUPS - GPB) // GPB
LAST = GROUPS + 2


def steps(eng, body):
    for j in range(-1, J0):
        body(At(j, 0))
    with eng.Fori(0, LOOPS) as i:
        for j in range(J0, J0 + GPB):
            body(At(j, i))
    for j in range(J0, J0 + LAST - (J0 + GPB * LOOPS) + 1):
        body(At(j, LOOPS))


def build(nc, x, w_in, ln_w, ln_b, conv_w, conv_b, conv_bc, a_log, d_skip, dt_bias, rms_w, w_out, out):
    from contextlib import ExitStack

    with ExitStack() as ctx:
        def sb(name, shape, dt=F32):
            return ctx.enter_context(nc.sbuf_tensor(name, [P, *shape], dt))

        sem = {k: ctx.enter_context(nc.semaphore(k)) for k in PER}
        dma = {k: [ctx.enter_context(nc.semaphore(f"{k}{r}")) for r in range(2)]
               for k in ("x_loaded", "xr_loaded", "out_stored", "hi_placed", "mid_placed", "lo_placed")}
        w_loaded = ctx.enter_context(nc.semaphore("w_loaded"))
        const_ready = ctx.enter_context(nc.semaphore("const_ready"))
        w_scaled = ctx.enter_context(nc.semaphore("w_scaled"))
        bias_done = ctx.enter_context(nc.semaphore("bias_done"))
        w_peak = ctx.enter_context(nc.semaphore("w_peak"))
        w_peak_moved = ctx.enter_context(nc.semaphore("w_peak_moved"))
        w_step = ctx.enter_context(nc.semaphore("w_step"))
        bias_ready = ctx.enter_context(nc.semaphore("bias_ready"))
        a_exp = ctx.enter_context(nc.semaphore("a_exp"))

        def bank(name, n=1):
            return ctx.enter_context(nc.psum_tensor(name, [P, n, 512], F32))

        big = bank("big", 2)
        dps = bank("dps", 2)
        tps = bank("tps")
        ydps = bank("ydps")
        yops = bank("yops")
        sm = bank("sm")

        w_sb = sb("w_sb", [2, KT, DPROJ], F16)
        wo_sb = sb("wo_sb", [2, XT, DIM], F16)
        lnw_sb, lnb_sb = sb("lnw_sb", [KT]), sb("lnb_sb", [KT])
        cw_sb, cb_sb = sb("cw_sb", [UT, TAPS]), sb("cb_sb", [UT])
        cbc_sb = sb("cbc_sb", [1])
        rms_sb = sb("rms_sb", [XT])
        alog_sb, a_sb, dsk_sb, dtb_sb = (sb(n, [HEADS]) for n in ("alog_sb", "a_sb", "dsk_sb", "dtb_sb"))
        ubias, zbias, dtbias = sb("ubias", [UT]), sb("zbias", [DINNER]), sb("dtbias", [HEADS])
        mean_w, ones, ident, tri, after = (sb(n, [P]) for n in ("mean_w", "ones", "ident", "tri", "after"))
        zeros = sb("zeros", [512])

        xb, xr = sb("xb", [2, KT, TOK]), sb("xr", [2, KT, TOK])
        xc, sq, rstd = sb("xc", [KT, TOK]), sb("sq", [KT, TOK]), sb("rstd", [TOK])
        xn = sb("xn", [4, 2, KT, TOK], F16)
        u = sb("u", [2, UT, ROWS + 2, PAD])
        acc = sb("acc", [UT, ROWS, IMG])
        pr = sb("pr", [2, len(AT), ROWS, IMG])
        xs = sb("xs", [2, XT, TOK])
        bt, ct = sb("bt", [2, TOK]), sb("ct", [2, TOK])
        z = sb("z", [2, CH, DINNER])
        room = z[:].rearrange("p s c d -> p (s c d)")
        after_w, after_wo = KT * DPROJ, KT * DPROJ + XT * DIM
        w_raw = room[:, 0:after_w].rearrange("p (k d) -> p k d", k=KT)
        wo_raw = room[:, after_w:after_wo].rearrange("p (k d) -> p k d", k=XT)
        lnb_bc = room[:, after_wo:after_wo + KT * P].rearrange("p (k q) -> p k q", k=KT)
        peak, peaks = sb("peak", [3, 2]), sb("peaks", [3])
        wscale, scale, unscale = sb("wscale", [2, 2]), sb("scale", [2]), sb("unscale", [2])
        dtv, dta, dt = (sb(n, [4, CH, HEADS]) for n in ("dtv", "dta", "dt"))
        da = sb("da", [2, CH, HEADS])
        dec = sb("dec", [4, 3, CH, HEADS])
        rest, pieces = sb("rest", [TOK]), sb("pieces", [PIECES, TOK], BF16)
        sums = sb("sums", [2, 2, TOK], BF16)
        of_head_s, of_head_q = sb("of_head_s", [HEADS, P], BF16), sb("of_head_q", [HEADS, P], BF16)
        em = sb("em", [2, HEADS, P])
        gm_btok = sb("gm_btok", [2, P + DSTATE])
        gm, btok = gm_btok[:, :, 0:P], gm_btok[:, :, P:P + DSTATE]
        xdt, xd, dx = sb("xdt", [2, DINNER]), sb("xd", [2, DINNER]), sb("dx", [2, DINNER])
        yb = sb("yb", [CH, DINNER])
        junk = sb("junk", [DINNER], BF16)
        rms = sb("rms", [2, 3])
        ynt = sb("ynt", [2, XT, TOK], F16)
        st, sd = sb("st", [2, DINNER]), sb("sd", [DINNER])

        block = ctx.enter_context(nc.Block())

        def count(name, n, k=None):
            per = PER[name]
            k = per - 1 if k is None else k
            if n.known is not None:
                return n.known * per + k + 1 if n.known >= 0 else 0
            assert n.j >= 0, (name, n.j)
            return n.i * (GPB * per) + (n.j * per + k + 1)

        def chunk(n, c):
            return (n + c // CH, c % CH)

        def landed(n):
            if n.known is not None and n.known < 0:
                return 0
            return n.i * (GPB // 2 * 16) + 16 * (n.j // 2 + 1)

        def transferred(n):
            if n.known is not None:
                return max(n.known + 1, 0) * 16
            return n.i * (GPB * 16) + (n.j + 1) * 16

        def heads(ap, w=HD):
            return ap.rearrange("p (h d) -> p h d", h=HEADS)

        def per_head(ap, w=HD, rows=P):
            return ap.unsqueeze(2).to_broadcast([rows, HEADS, w])

        U, O, Z = (lambda m: ("u", 0, m, "u_ready")), (lambda m: ("o", -3, m, "out_ready")), (
            lambda c: ("z", -1, c, "z_biased"))
        ACS = ("acs", -1, 0, "acs_rest")
        MEAN, VAR = ("mean", 1, 0, "centered"), ("var", 1, 0, "lnvar")
        FILL = [([Z(0)], [MEAN, Z(1)]), ([U(0), U(1)], [U(2), VAR]), ([U(3), Z(2)], [U(4), ACS]),
                ([Z(3)], [O(0), O(1)])]
        BIG = [use for pair in FILL for half in pair for use in half]
        NBIG = len(BIG)
        where = {(b[0], b[2]): q for q, b in enumerate(BIG)}

        def big_bank(t, what, part=0):
            return (t.j * NBIG + where[what, part]) % 2

        def big_free(eng, t, what, part=0):
            q = where[what, part] - 2
            s = t + (q // NBIG)
            kind, d, k, free = BIG[q % NBIG]
            if (s + d).exists:
                eng.wait_ge(sem[free], count(free, s + d, k))
            else:
                while (q // NBIG + t.known) >= -1:
                    q -= 2
                    s = t + (q // NBIG)
                    kind, d, k, free = BIG[q % NBIG]
                    if (s + d).exists:
                        eng.wait_ge(sem[free], count(free, s + d, k))
                        return

        @block.sync
        def _(sp):
            for dst, src in ((w_raw, w_in), (wo_raw, w_out), (lnw_sb, ln_w), (lnb_sb, ln_b), (cw_sb, conv_w),
                             (cb_sb, conv_b), (rms_sb, rms_w), (alog_sb, a_log), (dsk_sb, d_skip),
                             (dtb_sb, dt_bias)):
                sp.dma_start(dst if dst in (w_raw, wo_raw) else dst[:], src).then_inc(w_loaded, 16)
            sp.dma_start(cbc_sb[0:DSTATE, :], conv_bc).then_inc(w_loaded, 16)

            def image(dram, n):
                g = n.j % GPB
                return dram[n.i + n.j // GPB, :, :, g * TOK:(g + 1) * TOK]

            def load(n):
                if n.exists:
                    sp.wait_ge(sem["centered"], count("centered", n - 2))
                    sp.dma_start(xb[:, n.j % 2], image(x, n)).then_inc(dma["x_loaded"][n.j % 2], 16)

            def step(t):
                if t.known == -1:
                    load(t + 1)
                load(t + 2)
                n = t - 2
                if n.exists:
                    sp.wait_ge(dma["out_stored"][(n - 2).j % 2], landed(n - 2))
                    sp.dma_start(xr[:, n.j % 2], image(x, n)).then_inc(dma["xr_loaded"][n.j % 2], 16)
                n = t - 1
                if n.exists:
                    for name, ready, a in (("hi_placed", "acs_hi", 0), ("mid_placed", "acs_mid", 1),
                                           ("lo_placed", "acs_lo", 2)):
                        sp.wait_ge(sem[ready], count(ready, n))
                        for side in range(2):
                            sp.dma_start(sums[a * HEADS:(a + 1) * HEADS, side, n.j % 2, :],
                                         pieces[0:HEADS, a, :]).then_inc(dma[name][side], 16)
                n = t - 3
                if n.exists:
                    sp.wait_ge(sem["out_ready"], count("out_ready", n))
                    sp.dma_start(image(out, n), xr[:, n.j % 2]).then_inc(dma["out_stored"][n.j % 2], 16)

            steps(sp, step)
            for stored in dma["out_stored"]:
                sp.wait_ge(stored, GROUPS // 2 * 16)

        @block.tensor
        def _(pe):
            pe.wait_ge(const_ready, CONSTS)
            pe.wait_ge(w_loaded, 16 * 11)
            for m in range(UT):
                for k in range(KT):
                    last = pe.matmul(sm[:, 0, m:m + 1], w_raw[:, k, DINNER + m * P:DINNER + (m + 1) * P],
                                     lnb_sb[:, k:k + 1], start=k == 0, stop=k == KT - 1)
            last.then_inc(bias_done, 1)
            pe.wait_ge(w_scaled, 1)
            for lo, w, dst in ((0, DINNER, ydps[:, 0, :]), (DPROJ - HEADS, HEADS, yops[:, 0, 0:HEADS])):
                for k in range(KT):
                    last = pe.matmul(dst, lnb_bc[:, k, :], w_raw[:, k, lo:lo + w], start=k == 0, stop=k == KT - 1)
            last.then_inc(bias_done, 1)
            pe.wait_ge(w_peak, 5)
            pe.wait_ge(bias_ready, 1)
            pe.transpose(sm[0:2, 0, 0:P], peak[:, 2, :], ident[:]).then_inc(w_peak_moved, 1)
            pe.wait_ge(w_peak, 7)
            pe.matmul(sm[:, 0, 0:2], ones[0:2, :], peaks[0:2, 1:3], start=True, stop=True).then_inc(w_peak_moved, 1)
            pe.wait_ge(w_scaled, 4)

            def mean(t):
                n = t + 1
                if n.exists:
                    pe.wait_ge(dma["x_loaded"][n.j % 2], landed(n))
                    big_free(pe, t, "mean")
                    for k in range(KT):
                        last = pe.matmul(big[:, big_bank(t, "mean"), :], mean_w[:], xb[:, n.j % 2, k, :],
                                         start=k == 0, stop=k == KT - 1)
                    last.then_inc(sem["mean_done"], 1)

            def var(t):
                n = t + 1
                if n.exists:
                    pe.wait_ge(sem["squared"], count("squared", n))
                    big_free(pe, t, "var")
                    for k in range(KT):
                        last = pe.matmul(big[:, big_bank(t, "var"), :], mean_w[:], sq[:, k, :],
                                         start=k == 0, stop=k == KT - 1)
                    last.then_inc(sem["var_done"], 1)

            def project_u(t, m):
                if t.exists:
                    if m == 0:
                        pe.wait_ge(sem["xn_ready"], count("xn_ready", t))
                    big_free(pe, t, "u", m)
                    for i, (a, b) in enumerate(SPLIT):
                        for k in range(KT):
                            last = pe.matmul(big[:, big_bank(t, "u", m), :],
                                             w_sb[:, a, k, DINNER + m * P:DINNER + (m + 1) * P],
                                             xn[:, t.j % 4, b, k, :],
                                             start=i + k == 0, stop=i == len(SPLIT) - 1 and k == KT - 1)
                    last.then_inc(sem["u_done"], 1)

            def project_z(t, c):
                n = t - 1
                if n.exists:
                    big_free(pe, t, "z", c)
                    for i, (a, b) in enumerate(SPLIT):
                        for k in range(KT):
                            last = pe.matmul(big[:, big_bank(t, "z", c), :],
                                             xn[:, n.j % 4, b, k, c * P:(c + 1) * P], w_sb[:, a, k, 0:DINNER],
                                             start=i + k == 0, stop=i == len(SPLIT) - 1 and k == KT - 1)
                    last.then_inc(sem["z_done"], 1)

            def project_dt(t):
                if t.exists:
                    pe.wait_ge(sem["gb_ready"], count("gb_ready", t - 2, CH - 2))
                    if t.known is not None and 0 < t.known < 2:
                        pe.wait_ge(sem["dec_ready"], count("dec_ready", t - 1))
                    for c in range(CH):
                        for i, (a, b) in enumerate(SPLIT):
                            for k in range(KT):
                                last = pe.matmul(sm[:, 0, c * HEADS:(c + 1) * HEADS],
                                                 xn[:, t.j % 4, b, k, c * P:(c + 1) * P],
                                                 w_sb[:, a, k, DPROJ - HEADS:],
                                                 start=i + k == 0, stop=i == len(SPLIT) - 1 and k == KT - 1)
                    last.then_inc(sem["dt_done"], 1)

            def decays(t):
                n = t - 1
                if n.exists:
                    pe.wait_ge(sem["da_ready"], count("da_ready", n))
                    pe.wait_ge(sem["dt_biased"], count("dt_biased", n))
                    pe.wait_ge(sem["gb_ready"], count("gb_ready", *chunk(t - 2, -1)))
                    for k, w in enumerate((tri, after, ones)):
                        last = pe.matmul(sm[:, 0, 32 * k:32 * k + 32], w[:],
                                         da[:, n.j % 2], start=True, stop=True)
                    last.then_inc(sem["decay_done"], 1)

            def running_sum(t):
                n = t - 1
                if n.exists:
                    big_free(pe, t, "acs")
                    for c in range(CH):
                        last = pe.matmul(big[0:HEADS, big_bank(t, "acs"), c * P:(c + 1) * P],
                                         da[:, n.j % 2, c, :], tri[:], start=True, stop=True)
                    last.then_inc(sem["acs_done"], 1)

            def project_out(t, m):
                n = t - 3
                if n.exists:
                    if m == 0:
                        pe.wait_ge(sem["ynt_ready"], count("ynt_ready", n))
                    big_free(pe, t, "o", m)
                    for i, (a, b) in enumerate(SPLIT):
                        for k in range(XT):
                            last = pe.matmul(big[:, big_bank(t, "o", m), :], wo_sb[:, a, k, m * P:(m + 1) * P],
                                             ynt[:, b, k, :],
                                             start=i + k == 0, stop=i == len(SPLIT) - 1 and k == XT - 1)
                    last.then_inc(sem["o_done"], 1)

            def first(t, c):
                n, k = chunk(t - 2, c)
                if not n.exists:
                    return
                tok = slice(k * P, (k + 1) * P)
                if k == 0:
                    pe.wait_ge(sem["conv_ready"], count("conv_ready", n))
                pe.wait_ge(sem["e_ready"], count("e_ready", *chunk(n, k - 1)))
                if k == 0:
                    for name in ("hi_placed", "mid_placed", "lo_placed"):
                        for placed in dma[name]:
                            pe.wait_ge(placed, transferred(n))
                for j in range(2):
                    pe.matmul(dps[:, j, :], sums[:, 0, n.j % 2, tok],
                              of_head_s[:, 4 * j:4 * j + 4, :].rearrange("p h q -> p (h q)"), start=True, stop=False)
                    for h in range(4):
                        last = pe.matmul(dps[:, j, h * P:(h + 1) * P], of_head_q[:, 4 * j + h, :],
                                         sums[:, 1, n.j % 2, tok], start=False, stop=h == 3)
                last.then_inc(sem["d_done"], 1)
                if c == -1:
                    pe.wait_ge(sem["dt_biased"], count("dt_biased", t - 1 if (t - 1).exists else n))
                if c == 0:
                    pe.wait_ge(sem["dec_ready"], count("dec_ready", t - 1 if (t - 1).exists else n))
                pe.wait_ge(sem["gb_ready"], count("gb_ready", *chunk(n, k - 1)))
                pe.matmul(sm[:, 0, 0:P], bt[0:DSTATE, n.j % 2, tok], ct[0:DSTATE, n.j % 2, tok],
                          start=True, stop=True)
                pe.transpose(sm[:, 0, P:P + DSTATE], bt[0:DSTATE, n.j % 2, tok],
                             ident[0:DSTATE, 0:DSTATE]).then_inc(sem["gb_done"], 1)
                pe.wait_ge(sem["ynt_ready"], count("ynt_ready", *chunk(n, k - 3)))
                pe.wait_ge(sem["dx_ready"], count("dx_ready", *chunk(n, k - 1)))
                for j in range(XT):
                    last = pe.transpose(tps[:, 0, j * P:(j + 1) * P], xs[:, n.j % 2, j, tok], ident[:])
                last.then_inc(sem["xt_done"], 1)

            def off(t, c):
                n, k = chunk(t - 2, c - 1)
                if not n.exists:
                    return
                start = n.j % GPB == 0 and k == 0
                pe.wait_ge(sem["s_ready"], count("s_ready", *chunk(n, k - 1)))
                s = zeros if start else st[:, (k - 1) % 2]
                pe.matmul(yops[:, 0, :], ct[0:DSTATE, n.j % 2, k * P:(k + 1) * P], s[0:DSTATE, :],
                          start=True, stop=True).then_inc(sem["yoff_done"], 1)

            def diag(t, c):
                n, k = chunk(t - 2, c - 1)
                if not n.exists:
                    return
                pe.wait_ge(sem["m_ready"], count("m_ready", n, k))
                pe.wait_ge(sem["y_summed"], count("y_summed", *chunk(n, k - 1)))
                for h in range(HEADS):
                    last = pe.matmul(ydps[:, 0, h * HD:(h + 1) * HD], em[:, k % 2, h, :],
                                     xdt[:, k % 2, h * HD:(h + 1) * HD], start=True, stop=True)
                last.then_inc(sem["ydiag_done"], 1)

            def state(t, c):
                n, k = chunk(t - 2, c - 1)
                if not n.exists:
                    return
                pe.wait_ge(sem["xd_ready"], count("xd_ready", n, k))
                pe.wait_ge(sem["yoff_scaled"], count("yoff_scaled", n, k))
                pe.matmul(yops[0:DSTATE, 0, :], btok[:, k % 2, :], xd[:, k % 2, :],
                          start=True, stop=True).then_inc(sem["state_done"], 1)

            def turn(t, c):
                n, k = chunk(t - 2, c - 2)
                if not n.exists:
                    return
                pe.wait_ge(sem["yn_ready"], count("yn_ready", n, k))
                m, q = chunk(t - 2, c)
                if m.exists:
                    pe.wait_ge(sem["dx_ready"], count("dx_ready", m, q))
                else:
                    pe.wait_ge(sem["ynt_ready"], count("ynt_ready", *chunk(n, k - 1)))
                for j in range(XT):
                    last = pe.transpose(tps[:, 0, j * P:(j + 1) * P], yb[:, k, j * P:(j + 1) * P], ident[:])
                last.then_inc(sem["yt_done"], 1)

            def fill(t, uses):
                for what, _, part, _ in uses:
                    if what in ("mean", "var", "acs"):
                        {"mean": mean, "var": var, "acs": running_sum}[what](t)
                    else:
                        {"u": project_u, "o": project_out, "z": project_z}[what](t, part)

            def step(t):
                for c in range(CH):
                    off(t, c - 1)
                    fill(t, FILL[c][0])
                    if c == 1:
                        decays(t)
                    diag(t, c - 1)
                    first(t, c - 1)
                    state(t, c - 1)
                    fill(t, FILL[c][1])
                    if c == CH - 1:
                        project_dt(t)
                    turn(t, c - 1)

            steps(pe, step)

        @block.scalar
        def _(act):
            act.wait_ge(w_loaded, 16 * 11)
            act.activation(a_sb[:], alog_sb[:], ACT.Exp).then_inc(a_exp, 1)
            act.wait_ge(const_ready, CONSTS)
            act.wait_ge(w_scaled, 4)

            def square(t):
                n = t + 1
                if n.exists:
                    act.wait_ge(sem["centered"], count("centered", n))
                    act.wait_ge(sem["var_done"], count("var_done", n - 1))
                    act.activation(sq[:], xc[:], ACT.Square).then_inc(sem["squared"], 1)

            def rstd_of(t):
                n = t + 1
                if n.exists:
                    act.wait_ge(sem["var_done"], count("var_done", n))
                    act.wait_ge(sem["xc_scaled"], count("xc_scaled", n - 1))
                    act.activation(rstd[:], big[:, big_bank(t, "var"), :], ACT.Ln,
                                   bias=EPS / XSCALE ** 2, scale=1.0 / XSCALE ** 2).then_inc(sem["lnvar"], 1)
                    act.wait_ge(sem["lnvar"], count("lnvar", n))
                    act.activation(rstd[:], rstd[:], ACT.Exp, scale=-0.5).then_inc(sem["rstd_ready"], 1)

            def xn_upper(t):
                n = t + 1
                if n.exists:
                    act.wait_ge(sem["xc_scaled"], count("xc_scaled", n))
                    act.wait_ge(sem["z_done"], count("z_done", n - 4))
                    act.activation(xn[:, n.j % 4, 0], xc[:], ACT.Copy).then_inc(sem["xn_hi"], 1)

            def top(t):
                n = t
                if n.exists:
                    act.wait_ge(sem["conv_step"], count("conv_step", n - 2))
                    act.wait_ge(sem["u_ready"], count("u_ready", n - 1))
                    dst = u[:, n.j % 2, :, 0, 1:IMG + 1]
                    if n.j % GPB == 0:
                        src = zeros[:, 0:UT * IMG].rearrange("p (m w) -> p m w", m=UT)
                    else:
                        src = u[:, (n.j - 1) % 2, :, ROWS, 1:IMG + 1]
                    act.activation(dst, src, ACT.Copy).then_inc(sem["top_halo"], 1)

            def u_rows(t, m):
                n = t
                if n.exists:
                    act.wait_ge(sem["u_done"], count("u_done", n, m))
                if (n - 1).exists:
                    dst = u[:, (n.j - 1) % 2, m, ROWS + 1, 1:IMG + 1]
                    if n.j % GPB == 0:
                        i = act.activation(dst, zeros[:, 0:IMG], ACT.Copy)
                    else:
                        i = act.activation(dst, big[:, big_bank(t, "u", m), 0:IMG], ACT.Identity,
                                           bias=ubias[:, m:m + 1])
                    i.then_inc(sem["bottom_halo"], 1)
                elif n.known == 0:
                    act.activation(junk[:, 0:IMG], zeros[:, 0:IMG], ACT.Copy).then_inc(sem["bottom_halo"], 1)
                    if m < UT - 1:
                        act.wait_ge(sem["bottom_halo"], count("bottom_halo", n, m))
                if n.exists:
                    act.activation(u[:, n.j % 2, m, 1:ROWS + 1, 1:IMG + 1],
                                   big[:, big_bank(t, "u", m), :].rearrange("p (r w) -> p r w", r=ROWS),
                                   ACT.Identity, bias=ubias[:, m:m + 1]).then_inc(sem["u_ready"], 1)

            def softplus(t):
                n = t
                if n.exists:
                    act.wait_ge(sem["dt_biased"], count("dt_biased", n))
                    v, a = dtv[:, n.j % 4], dta[:, n.j % 4]
                    act.activation(a, v, ACT.Abs).then_inc(sem["dt_abs"], 1)
                    act.wait_ge(sem["dt_abs"], count("dt_abs", n))
                    act.activation(a, a, ACT.Exp, scale=-1.0).then_inc(sem["dt_exp"], 1)
                    act.wait_ge(sem["dt_exp"], count("dt_exp", n))
                    act.activation(a, a, ACT.Ln, bias=1.0).then_inc(sem["dt_log"], 1)

            def decays(t):
                n = t - 1
                if n.exists:
                    act.wait_ge(sem["decay_done"], count("decay_done", n))
                    act.activation(dec[:, n.j % 4].rearrange("p k c h -> p (k c h)"), sm[:, 0, 0:96],
                                   ACT.Exp).then_inc(sem["dec_ready"], 1)

            def split_hi(t):
                n = t - 1
                if n.exists:
                    act.wait_ge(sem["acs_done"], count("acs_done", n))
                    for placed in dma["hi_placed"]:
                        act.wait_ge(placed, transferred(n - 1))
                    act.wait_ge(sem["d_done"], count("d_done", n - 2))
                    act.activation(pieces[0:HEADS, 0, :], big[0:HEADS, big_bank(t, "acs"), :], ACT.Copy).then_inc(
                        sem["acs_hi"], 1)

            def split_mid(t):
                n = t - 1
                if n.exists:
                    act.wait_ge(sem["acs_rest"], count("acs_rest", n))
                    for placed in dma["mid_placed"]:
                        act.wait_ge(placed, transferred(n - 1))
                    act.activation(pieces[0:HEADS, 1, :], rest[0:HEADS, :], ACT.Copy).then_inc(sem["acs_mid"], 1)

            def small(t, c):
                n, k = chunk(t - 2, c)
                if n.exists:
                    act.wait_ge(sem["gb_done"], count("gb_done", n, k))
                    act.wait_ge(sem["m_ready"], count("m_ready", *chunk(n, k - 2)))
                    act.wait_ge(sem["state_done"], count("state_done", *chunk(n, k - 2)))
                    act.activation(gm_btok[:, k % 2, :], sm[:, 0, 0:P + DSTATE], ACT.Copy).then_inc(
                        sem["gb_ready"], 1)

            def exps(t, c):
                n, k = chunk(t - 2, c)
                if n.exists:
                    act.wait_ge(sem["d_done"], count("d_done", n, k))
                    act.wait_ge(sem["ydiag_done"], count("ydiag_done", *chunk(n, k - 2)))
                    act.activation(em[:, k % 2].rearrange("p h q -> p (h q)"),
                                   dps[:].rearrange("p k q -> p (k q)"), ACT.Exp).then_inc(sem["e_ready"], 1)

            def rms_of(t, c):
                n, k = chunk(t - 2, c - 2)
                if n.exists:
                    act.wait_ge(sem["y_gated"], count("y_gated", n, k))
                    act.wait_ge(sem["yn_ready"], count("yn_ready", *chunk(n, k - 2)))
                    act.wait_ge(sem["ss_ready"], count("ss_ready", *chunk(n, k - 1)))
                    act.activation(junk[:], yb[:, k, :], ACT.Square,
                                   accum_out=rms[:, k % 2, 0:1]).then_inc(sem["ss_ready"], 1)
                    act.wait_ge(sem["ss_ready"], count("ss_ready", n, k))
                    act.activation(rms[:, k % 2, 1:2], rms[:, k % 2, 0:1], ACT.Ln,
                                   bias=EPS / YSCALE ** 2, scale=1.0 / (DINNER * YSCALE ** 2)).then_inc(sem["rms_log"], 1)
                    act.wait_ge(sem["rms_log"], count("rms_log", n, k))
                    act.activation(rms[:, k % 2, 2:3], rms[:, k % 2, 1:2], ACT.Exp, scale=-0.5).then_inc(
                        sem["rms_ready"], 1)

            def normalise(t, c):
                n, k = chunk(t - 2, c - 2)
                if n.exists:
                    act.wait_ge(sem["rms_ready"], count("rms_ready", n, k))
                    act.activation(yb[:, k, :], yb[:, k, :], ACT.Copy, scale=rms[:, k % 2, 2:3]).then_inc(
                        sem["yn_ready"], 1)

            def turned(t, c):
                n, k = chunk(t - 2, c - 3)
                if n.exists:
                    act.wait_ge(sem["yt_done"], count("yt_done", n, k))
                    if k == 0:
                        act.wait_ge(sem["o_done"], count("o_done", n - 1))
                    act.activation(ynt[:, 0, :, k * P:(k + 1) * P],
                                   tps[:, 0, :].rearrange("p (j q) -> p j q", j=XT),
                                   ACT.Copy).then_inc(sem["yt_hi"], 1)

            def silu_x(t, tiles):
                n = t - 2
                if not n.exists:
                    return
                act.wait_ge(sem["yoff_done"], count("yoff_done", n - 2))
                for m in tiles:
                    if m in VT:
                        act.wait_ge(sem["conv_step"], count("conv_step", n, (TAPS - 1) * len(VT) + m))
                    else:
                        act.wait_ge(sem["tap_added"], count("tap_added", n))
                    act.activation(xs[:, n.j % 2, m, :], acc[:, m].rearrange("p r w -> p (r w)"), ACT.Silu,
                                   bias=cb_sb[:, m:m + 1]).then_inc(sem["conv_ready"], 1)

            def silu_bc(t):
                n = t - 2
                if not n.exists:
                    return
                act.wait_ge(sem["tap_added"], count("tap_added", n))
                for dst, rows, bias in ((bt, slice(0, DSTATE), cb_sb[0:DSTATE, XT:UT]),
                                        (ct, slice(DSTATE, P), cb_sb[DSTATE:P, XT:UT])):
                    act.activation(dst[0:DSTATE, n.j % 2, :], acc[rows, XT].rearrange("p r w -> p (r w)"),
                                   ACT.Silu, bias=cbc_sb[0:DSTATE, :] if dst is ct else bias).then_inc(
                                       sem["conv_ready"], 1)

            def silu_z(t, c):
                n = t - 2
                if n.exists:
                    act.wait_ge(sem["z_biased"], count("z_biased", n, c))
                    act.activation(z[:, n.j % 2, c, :], z[:, n.j % 2, c, :], ACT.Silu,
                                   scale=unscale[:, 0:1]).then_inc(sem["z_ready"], 1)

            def taps(t, lo, hi):
                n = t - 1
                if not n.exists:
                    return
                for q in range(lo, hi):
                    tap, a = divmod(q, len(AT))
                    m = AT[a]
                    dy, dx_ = divmod(tap, 3)
                    if q == 0:
                        act.wait_ge(sem["top_halo"], count("top_halo", n))
                        act.wait_ge(sem["u_ready"], count("u_ready", n))
                        act.wait_ge(sem["conv_ready"], count("conv_ready", n - 1))
                    if dy == 2 and dx_ == 0:
                        act.wait_ge(sem["bottom_halo"], count("bottom_halo", n + 1, m))
                    if tap > 2:
                        act.wait_ge(sem["tap_added"], count("tap_added", n, q - 3 * len(AT)))
                    elif tap:
                        act.wait_ge(sem["tap_added"], count("tap_added", n - 1))
                    dst = pr[:, tap % 2, a] if tap else acc[:, m]
                    act.activation(dst, u[:, n.j % 2, m, dy:dy + ROWS, dx_:dx_ + IMG], ACT.Copy,
                                   scale=cw_sb[:, m, tap:tap + 1]).then_inc(sem["tap_made"], 1)

            def step(t):
                for c in range(CH):
                    if c:
                        turned(t, c - 1)
                    rms_of(t, c - 1)
                    normalise(t, c - 1)
                    if c == 3:
                        xn_upper(t)
                    if c == 0:
                        softplus(t - 1)
                        turned(t, c - 1)
                        for k in range(CH):
                            silu_z(t, k)
                        silu_x(t, range(XT))
                        silu_bc(t)
                        act.preload_act_table_set("natural_log_exp_and_others")
                    if c == 1:
                        decays(t)
                    for what, _, part, _ in FILL[c][0]:
                        if what == "u":
                            if part == 0:
                                top(t)
                            u_rows(t, part)
                    exps(t, c - 1)
                    small(t, c - 1)
                    if c == 3:
                        split_mid(t)
                    taps(t, *((0, 0), (3, 5), (7, 11), (13, 15))[c])
                    for what, _, part, _ in FILL[c][1]:
                        if what == "u":
                            u_rows(t, part)
                        if what == "var":
                            rstd_of(t)
                        if what == "acs":
                            split_hi(t)
                    taps(t, *((0, 3), (5, 7), (11, 13), (15, 18))[c])
                    if c == 0:
                        square(t)

            steps(act, step)

        @block.vector
        def _(dve):
            dve.wait_ge(w_loaded, 16 * 11)
            for k in range(KT):
                i = dve.tensor_copy(lnb_bc[:, k, :], lnb_sb[:, k:k + 1].to_broadcast([P, P]))
            i.then_inc(w_scaled, 1)
            dve.wait_ge(bias_done, 2)
            for k in range(KT):
                i = dve.tensor_scalar(w_raw[:, k, :], w_raw[:, k, :], lnw_sb[:, k:k + 1], None, ALU.mult)
            i.then_inc(w_scaled, 1)
            for k in range(XT):
                i = dve.tensor_scalar(wo_raw[:, k, :], wo_raw[:, k, :], rms_sb[:, k:k + 1], None, ALU.mult)
            i.then_inc(w_scaled, 1)
            dve.tensor_copy(ubias[:], sm[:, 0, 0:UT]).then_inc(bias_ready, 1)
            dve.tensor_copy(zbias[:], ydps[:, 0, :]).then_inc(bias_ready, 1)
            dve.tensor_tensor(dtbias[:], dtb_sb[:], yops[:, 0, 0:HEADS], ALU.add).then_inc(bias_ready, 1)
            dve.wait_ge(w_scaled, 3)
            for p, (lo, hi) in enumerate(((0, after_w), (after_w, after_wo))):
                for a, op in enumerate((ALU.max, ALU.min)):
                    dve.tensor_reduce(peak[:, a, p:p + 1], room[:, lo:hi], mybir.AxisListType.X, op).then_inc(
                        w_peak, 1)
            dve.wait_ge(w_peak, 4)
            dve.scalar_tensor_tensor(peak[:, 2, :], peak[:, 1, :], -1.0, peak[:, 0, :], ALU.mult, ALU.max).then_inc(
                w_peak, 1)
            dve.wait_ge(w_peak_moved, 1)
            dve.tensor_reduce(peaks[0:2, 0:1], sm[0:2, 0, 0:P], mybir.AxisListType.X, ALU.max).then_inc(w_peak, 1)
            dve.wait_ge(w_peak, 6)
            dve.tensor_scalar(peaks[0:2, 1:3], ident[0:2, 0:2], peaks[0:2, 0:1], None, ALU.mult).then_inc(w_peak, 1)
            dve.wait_ge(w_peak_moved, 2)
            dve.tensor_scalar(wscale[:, 0], sm[:, 0, 0:2], 1.0 / WMAX, TINY, ALU.mult, ALU.max).then_inc(w_step, 1)
            dve.wait_ge(w_step, 1)
            dve.reciprocal(wscale[:, 1], wscale[:, 0]).then_inc(w_step, 1)
            dve.wait_ge(w_step, 2)
            for p, by in enumerate((XSCALE, YSCALE)):
                i = dve.tensor_scalar(scale[:, p:p + 1], wscale[:, 1, p:p + 1], by, None, ALU.mult)
            i.then_inc(w_step, 1)
            dve.wait_ge(w_step, 3)
            dve.reciprocal(unscale[:], scale[:]).then_inc(w_step, 1)
            dve.wait_ge(w_step, 4)
            for p, (raw, dst) in enumerate(((w_raw, w_sb), (wo_raw, wo_sb))):
                dve.tensor_scalar(raw, raw, wscale[:, 1, p:p + 1], None, ALU.mult).then_inc(w_step, 1)
                dve.wait_ge(w_step, 5 + 3 * p)
                dve.tensor_copy(dst[:, 0], raw).then_inc(w_step, 1)
                dve.wait_ge(w_step, 6 + 3 * p)
                dve.tensor_tensor(dst[:, 1], raw, dst[:, 0], ALU.subtract).then_inc(w_step, 1)
            dve.tensor_scalar(ubias[:], ubias[:], scale[:, 0:1], None, ALU.mult).then_inc(w_step, 1)
            dve.tensor_scalar(zbias[:], zbias[:], scale[:, 0:1], None, ALU.mult).then_inc(w_step, 1)
            dve.tensor_scalar(cw_sb[:].rearrange("p m a -> p (m a)"), cw_sb[:].rearrange("p m a -> p (m a)"),
                              unscale[:, 0:1], None, ALU.mult).then_inc(w_step, 1)
            dve.wait_ge(w_step, 13)
            dve.wait_ge(a_exp, 1)
            dve.tensor_scalar(a_sb[:], a_sb[:], -1.0, None, ALU.mult).then_inc(bias_ready, 1)
            dve.wait_ge(bias_ready, 4)
            dve.nop().then_inc(w_scaled, 1)
            dve.wait_ge(const_ready, CONSTS)

            def center(t):
                n = t + 1
                if n.exists:
                    dve.wait_ge(sem["mean_done"], count("mean_done", n))
                    dve.wait_ge(sem["xn_ready"], count("xn_ready", n - 1))
                    dve.tensor_tensor(xc[:], xb[:, n.j % 2],
                                      big[:, big_bank(t, "mean"), :].unsqueeze(1).to_broadcast([P, KT, TOK]),
                                      ALU.subtract).then_inc(sem["centered"], 1)

            def z_bias(t, c):
                n = t - 1
                if n.exists:
                    dve.wait_ge(sem["z_done"], count("z_done", n, c))
                    dve.wait_ge(sem["y_gated"], count("y_gated", n - 2, c))
                    dve.tensor_tensor(z[:, n.j % 2, c, :], big[:, big_bank(t, "z", c), :], zbias[:],
                                      ALU.add).then_inc(sem["z_biased"], 1)

            def dt_bias_add(t):
                n = t
                if n.exists:
                    dve.wait_ge(sem["dt_done"], count("dt_done", n))
                    dve.scalar_tensor_tensor(dtv[:, n.j % 4], sm[:, 0, 0:32].rearrange("p (c h) -> p c h", c=CH),
                                             unscale[:, 0:1],
                                             dtbias[:].unsqueeze(1).to_broadcast([P, CH, HEADS]),
                                             ALU.mult, ALU.add).then_inc(sem["dt_biased"], 1)

            def dt_end(t):
                n = t
                if n.exists:
                    dve.wait_ge(sem["dt_log"], count("dt_log", n))
                    dve.scalar_tensor_tensor(dt[:, n.j % 4], dtv[:, n.j % 4], 0.0, dta[:, n.j % 4],
                                             ALU.max, ALU.add).then_inc(sem["dt_ready"], 1)
                    dve.wait_ge(sem["dt_ready"], count("dt_ready", n))
                    dve.tensor_tensor(da[:, n.j % 2], dt[:, n.j % 4],
                                      a_sb[:].unsqueeze(1).to_broadcast([P, CH, HEADS]),
                                      ALU.mult).then_inc(sem["da_ready"], 1)

            def x_tokens(t, c):
                n, k = chunk(t - 2, c)
                if n.exists:
                    dve.wait_ge(sem["xt_done"], count("xt_done", n, k))
                    dve.wait_ge(sem["xd_ready"], count("xd_ready", *chunk(n, k - 2)))
                    dve.wait_ge(sem["ydiag_done"], count("ydiag_done", *chunk(n, k - 2)))
                    dve.tensor_tensor(heads(xdt[:, k % 2, :]), heads(tps[:, 0, :]),
                                      per_head(dt[:, n.j % 4, k, :]), ALU.mult).then_inc(sem["xdt_ready"], 1)
                    dve.wait_ge(sem["yd_added"], count("yd_added", *chunk(n, k - 2)))
                    dve.tensor_tensor(heads(dx[:, k % 2, :]), heads(tps[:, 0, :]), per_head(dsk_sb[:]),
                                      ALU.mult).then_inc(sem["dx_ready"], 1)

            def masked(t, c):
                n, k = chunk(t - 2, c)
                if n.exists:
                    dve.wait_ge(sem["e_ready"], count("e_ready", n, k))
                    dve.wait_ge(sem["gb_ready"], count("gb_ready", n, k))
                    dve.tensor_tensor(em[:, k % 2], em[:, k % 2],
                                      gm[:, k % 2, :].unsqueeze(1).to_broadcast([P, HEADS, P]),
                                      ALU.mult).then_inc(sem["m_ready"], 1)

            def off_scale(t, c):
                n, k = chunk(t - 2, c - 1)
                if n.exists:
                    dve.wait_ge(sem["yoff_done"], count("yoff_done", n, k))
                    dve.wait_ge(sem["yt_done"], count("yt_done", *chunk(n, k - 4)))
                    dve.tensor_tensor(heads(yb[:, k, :]), heads(yops[:, 0, :]),
                                      per_head(dec[:, n.j % 4, 0, k, :]), ALU.mult).then_inc(sem["yoff_scaled"], 1)

            def sum_y(t, c):
                n, k = chunk(t - 2, c - 1)
                if n.exists:
                    dve.wait_ge(sem["ydiag_done"], count("ydiag_done", n, k))
                    dve.wait_ge(sem["yd_added"], count("yd_added", n, k))
                    dve.tensor_tensor(yb[:, k, :], yb[:, k, :], ydps[:, 0, :],
                                      ALU.add).then_inc(sem["y_summed"], 1)

            def split_rest(t):
                n = t - 1
                if n.exists:
                    dve.wait_ge(sem["acs_hi"], count("acs_hi", n))
                    dve.tensor_tensor(rest[0:HEADS, :], big[0:HEADS, big_bank(t, "acs"), :],
                                      pieces[0:HEADS, 0, :], ALU.subtract).then_inc(sem["acs_rest"], 1)

            def split_lo(t):
                n = t - 1
                if n.exists:
                    dve.wait_ge(sem["acs_mid"], count("acs_mid", n))
                    for placed in dma["lo_placed"]:
                        dve.wait_ge(placed, transferred(n - 1))
                    dve.tensor_tensor(pieces[0:HEADS, 2, :], rest[0:HEADS, :], pieces[0:HEADS, 1, :],
                                      ALU.subtract).then_inc(sem["acs_lo"], 1)

            def new_state(t, c):
                n, k = chunk(t - 2, c - 1)
                if n.exists:
                    dve.wait_ge(sem["state_done"], count("state_done", n, k))
                    dve.wait_ge(sem["s_decayed"], count("s_decayed", n, k))
                    dve.tensor_tensor(st[0:DSTATE, k % 2, :], sd[0:DSTATE, :], yops[0:DSTATE, 0, :],
                                      ALU.add).then_inc(sem["s_ready"], 1)

            def turned_rest(t, c):
                n, k = chunk(t - 2, c - 3)
                if n.exists:
                    dve.wait_ge(sem["yt_hi"], count("yt_hi", n, k))
                    tok = slice(k * P, (k + 1) * P)
                    dve.tensor_tensor(ynt[:, 1, :, tok], tps[:, 0, :].rearrange("p (j q) -> p j q", j=XT),
                                      ynt[:, 0, :, tok], ALU.subtract).then_inc(sem["ynt_ready"], 1)

            def finish(t, m):
                n = t - 3
                if n.exists:
                    dve.wait_ge(sem["o_done"], count("o_done", n, m))
                    if m == 0:
                        dve.wait_ge(dma["xr_loaded"][n.j % 2], landed(n))
                    dve.scalar_tensor_tensor(xr[:, n.j % 2, m, :], big[:, big_bank(t, "o", m), :],
                                             unscale[:, 1:2], xr[:, n.j % 2, m, :],
                                             ALU.mult, ALU.add).then_inc(sem["out_ready"], 1)

            def convolve(t, lo, hi):
                n = t - 1
                if not n.exists:
                    return
                for q in range(lo, hi):
                    tap, m = divmod(q, len(VT))
                    m = VT[m]
                    dy, dx_ = divmod(tap, 3)
                    if q == 0:
                        dve.wait_ge(sem["top_halo"], count("top_halo", n))
                        dve.wait_ge(sem["u_ready"], count("u_ready", n))
                    if dy == 2 and dx_ == 0:
                        dve.wait_ge(sem["bottom_halo"], count("bottom_halo", n + 1, m))
                    src = u[:, n.j % 2, m, dy:dy + ROWS, dx_:dx_ + IMG]
                    w = cw_sb[:, m, tap:tap + 1]
                    if tap:
                        dve.wait_ge(sem["conv_step"], count("conv_step", n, q - len(VT)))
                    else:
                        dve.wait_ge(sem["conv_ready"], count("conv_ready", n - 1, m))
                    if tap:
                        i = dve.scalar_tensor_tensor(acc[:, m], src, w, acc[:, m], ALU.mult, ALU.add)
                    else:
                        i = dve.tensor_scalar(acc[:, m], src, w, None, ALU.mult)
                    i.then_inc(sem["conv_step"], 1)

            def step(t):
                for c in range(CH):
                    off_scale(t, c - 1)
                    turned_rest(t, c - 1)
                    if c != 1:
                        z_bias(t, c)
                    convolve(t, *((0, 0), (3, 7), (11, 13), (18, 21))[c])
                    sum_y(t, c - 1)
                    x_tokens(t, c - 1)
                    new_state(t, c - 1)
                    if c == 0:
                        dt_end(t - 1)
                        center(t)
                        z_bias(t, 1)
                    convolve(t, *((0, 3), (7, 7), (13, 14), (21, 22))[c])
                    if c == 2:
                        split_rest(t)
                    if c == 3:
                        split_lo(t)
                        finish(t, 0)
                        convolve(t, 22, 24)
                        finish(t, 1)
                        dt_bias_add(t)
                    masked(t, c - 1)
                    convolve(t, *((0, 0), (7, 11), (14, 18), (24, 27))[c])

            steps(dve, step)

        @block.gpsimd
        def _(pool):
            pool.memset(mean_w[:], 1.0 / DIM).then_inc(const_ready, 1)
            pool.memset(ones[:], 1.0).then_inc(const_ready, 1)
            pool.memset(zeros[:], 0.0).then_inc(const_ready, 1)
            pool.memset(u[:], 0.0).then_inc(const_ready, 1)
            for c in (ident, tri, after):
                last = pool.memset(c[:], 1.0)
            last.then_inc(const_ready, 1)
            pool.wait_ge(const_ready, 5)
            pool.affine_select(out=ident[:], in_=ident[:], compare_op=ALU.is_equal, fill=0.0, base=0,
                               pattern=[[-1, P]], channel_multiplier=1).then_inc(const_ready, 1)
            pool.affine_select(out=tri[:], in_=tri[:], compare_op=ALU.is_ge, fill=0.0, base=0,
                               pattern=[[1, P]], channel_multiplier=-1).then_inc(const_ready, 1)
            pool.affine_select(out=after[:], in_=after[:], compare_op=ALU.is_gt, fill=0.0, base=0,
                               pattern=[[-1, P]], channel_multiplier=1).then_inc(const_ready, 1)
            pool.memset(yb[:], 0.0).then_inc(const_ready, 1)
            pool.wait_ge(const_ready, 9)
            pool.memset(junk[:], 0.0).then_inc(const_ready, 1)
            pool.memset(sums[:, 0], 1.0).then_inc(const_ready, 1)
            pool.memset(sums[:, 1], NEVER).then_inc(const_ready, 1)
            pool.memset(of_head_s[:], NEVER).then_inc(const_ready, 1)
            pool.memset(of_head_q[:], 0.0).then_inc(const_ready, 1)
            pool.wait_ge(const_ready, 14)

            def select(tile, compare_op, fill, base, pattern):
                pool.affine_select(out=tile, in_=tile, compare_op=compare_op, fill=fill, base=base,
                                   pattern=pattern, channel_multiplier=1).then_inc(const_ready, 1)

            taken = PIECES * HEADS
            by_token, by_head = [[0, 2 * CH], [-1, P]], [[0, HEADS], [-1, P]]
            select(sums[:, 0].rearrange("p k (c q) -> p (k c) q", q=P), ALU.is_equal, 0.0, 0, by_token)
            select(sums[:, 1].rearrange("p k (c q) -> p (k c) q", q=P), ALU.is_gt, 0.0, -taken, by_token)
            select(of_head_s[:], ALU.is_gt, 0.0, 0, by_head)
            select(of_head_q[:], ALU.not_equal, 1.0, -taken, by_head)
            pool.wait_ge(const_ready, 18)
            select(of_head_s[:], ALU.is_ge, 0.0, -taken, [[0, HEADS], [0, P]])
            for a in range(PIECES):
                pool.wait_ge(const_ready, 19 + 2 * a)
                select(of_head_s[:], ALU.not_equal, -1.0, -HEADS * a, [[-1, HEADS], [0, P]])
                select(of_head_q[:], ALU.not_equal, 1.0, -HEADS * a, [[-1, HEADS], [0, P]])
            pool.wait_ge(const_ready, CONSTS)
            pool.wait_ge(w_loaded, 16 * 11)

            def product(out_, a, b, name, op=ALU.mult):
                pool.tensor_tensor(out_, a, b, op).then_inc(sem[name], 1)

            def norm(t):
                n = t + 1
                if n.exists:
                    pool.wait_ge(sem["rstd_ready"], count("rstd_ready", n))
                    product(xc[:], xc[:], rstd[:].unsqueeze(1).to_broadcast([P, KT, TOK]), "xc_scaled")

            def xn_lower(t):
                n = t + 1
                if n.exists:
                    pool.wait_ge(sem["xn_hi"], count("xn_hi", n))
                    product(xn[:, n.j % 4, 1], xc[:], xn[:, n.j % 4, 0], "xn_ready", ALU.subtract)

            def skip(t, c):
                n, k = chunk(t - 2, c - 1)
                if n.exists:
                    pool.wait_ge(sem["yoff_scaled"], count("yoff_scaled", n, k))
                    product(yb[:, k, :], yb[:, k, :], dx[:, k % 2, :], "yd_added", ALU.add)

            def decayed_x(t, c):
                n, k = chunk(t - 2, c)
                if n.exists:
                    pool.wait_ge(sem["xdt_ready"], count("xdt_ready", n, k))
                    pool.wait_ge(sem["state_done"], count("state_done", *chunk(n, k - 2)))
                    product(heads(xd[:, k % 2, :]), heads(xdt[:, k % 2, :]), per_head(dec[:, n.j % 4, 1, k, :]),
                            "xd_ready")

            def decayed_state(t, c):
                n, k = chunk(t - 2, c - 1)
                if n.exists:
                    pool.wait_ge(sem["s_ready"], count("s_ready", *chunk(n, k - 1)))
                    start = n.j % GPB == 0 and k == 0
                    s = zeros[0:DSTATE, :] if start else st[0:DSTATE, (k - 1) % 2, :]
                    product(heads(sd[0:DSTATE, :]), heads(s), per_head(dec[0:DSTATE, n.j % 4, 2, k, :], rows=DSTATE),
                            "s_decayed")

            def gate(t, c):
                n, k = chunk(t - 2, c - 1)
                if n.exists:
                    pool.wait_ge(sem["y_summed"], count("y_summed", n, k))
                    pool.wait_ge(sem["z_ready"], count("z_ready", n, k))
                    product(yb[:, k, :], yb[:, k, :], z[:, n.j % 2, k, :], "y_gated")

            def add_taps(t, lo, hi):
                n = t - 1
                if n.exists:
                    for q in range(lo, hi):
                        tap, a = divmod(q, len(AT))
                        pool.wait_ge(sem["tap_made"], count("tap_made", n, q + len(AT)))
                        if tap:
                            pool.wait_ge(sem["tap_added"], count("tap_added", n, q - len(AT)))
                        product(acc[:, AT[a]], acc[:, AT[a]], pr[:, (tap + 1) % 2, a], "tap_added", ALU.add)

            def step(t):
                for c in range(CH):
                    skip(t, c - 1)
                    decayed_state(t, c - 1)
                    if c == 0:
                        xn_lower(t - 1)
                    add_taps(t, *((0, 0), (0, 3), (5, 7), (9, 12))[c])
                    gate(t, c - 1)
                    if c == 2:
                        norm(t)
                    decayed_x(t, c - 1)
                    add_taps(t, *((0, 0), (3, 5), (7, 9), (12, 16))[c])

            steps(pool, step)


def kernel(x, L0_conv_ln_w, L0_conv_ln_b, L0_conv_in_proj_w, L0_conv_conv_w, L0_conv_conv_b, L0_conv_A_log,
           L0_conv_D, L0_conv_dt_bias, L0_conv_rms_w, L0_conv_out_proj_w):
    import concourse.bacc as bacc
    from concourse.bass_utils import run_bass_kernel_spmd

    def rows(a, n):
        a = np.asarray(a)
        return np.ascontiguousarray(np.moveaxis(a.reshape(n, P, *a.shape[1:]), 0, 1))

    def everywhere(a):
        return np.ascontiguousarray(np.broadcast_to(np.asarray(a), (P, a.shape[0])))

    xv = np.ascontiguousarray(np.asarray(x).reshape(B, KT, P, IMG * IMG).transpose(0, 2, 1, 3))
    arrays = {
        "x": xv,
        "w_in": rows(np.asarray(L0_conv_in_proj_w).T, KT),
        "ln_w": rows(L0_conv_ln_w, KT), "ln_b": rows(L0_conv_ln_b, KT),
        "conv_w": rows(np.asarray(L0_conv_conv_w).reshape(UT * P, TAPS), UT), "conv_b": rows(L0_conv_conv_b, UT),
        "conv_bc": np.ascontiguousarray(np.asarray(L0_conv_conv_b)[-DSTATE:, None]),
        "a_log": everywhere(L0_conv_A_log), "d_skip": everywhere(L0_conv_D),
        "dt_bias": everywhere(L0_conv_dt_bias),
        "rms_w": rows(L0_conv_rms_w, XT), "w_out": rows(np.asarray(L0_conv_out_proj_w).T, XT),
    }
    nc = bacc.Bacc("TRN2", target_bir_lowering=False, num_devices=1)
    args = [nc.dram_tensor(f"in_{k}", a.shape, mybir.dt.from_np(a.dtype), kind="ExternalInput").ap()
            for k, a in arrays.items()]
    out = nc.dram_tensor("out", xv.shape, F32, kind="ExternalOutput").ap()
    build(nc, *args, out)
    r = run_bass_kernel_spmd(nc, [{f"in_{k}": a for k, a in arrays.items()}], core_ids=[0])
    got = r.results[0]["out"]
    return np.ascontiguousarray(got.transpose(0, 2, 1, 3)).reshape(B, DIM, IMG, IMG)
```
